# Optimizing a Trainium2 kernel written in Bass

```python
import numpy as np
import jax
import jax.numpy as jnp

def _softmax(x, axis=-1):
    return jax.nn.softmax(x, axis=axis)

def _gelu(x):
    return jax.nn.gelu(x, approximate=True)

def _silu(x):
    return jax.nn.silu(x)

def _sigmoid(x):
    return jax.nn.sigmoid(x)

def _layernorm(x, axis=-1, eps=1e-05):
    m = jnp.mean(x, axis=axis, keepdims=True)
    v = jnp.var(x, axis=axis, keepdims=True)
    return (x - m) / jnp.sqrt(v + eps)

def _scatter_add(tgt, idx, src, axis=0):
    return tgt.at[idx].add(src)

def _segment_sum(src, seg, n):
    return jax.ops.segment_sum(src, seg, n)
kernel_name = 'mk_hybrid_d1_jaxref_r8_6e7c26'

def setup_inputs(seed: int=0):
    np.random.seed(seed)
    _w = jnp.asarray

    def _L0_attn_a_setup():
        import jax, jax.numpy as jnp
        import numpy as np
        EMBED = 128
        HEADS = 16
        HEAD_DIM = EMBED // HEADS
        B, T = (2, 256)
        ROPE_THETA = 10000.0

        def _rope(x):
            D = x.shape[-1]
            inv_freq = 1.0 / ROPE_THETA ** (jnp.arange(0, D, 2, dtype=jnp.float32) / D)
            freqs = jnp.arange(x.shape[2], dtype=jnp.float32)[:, None] * inv_freq[None, :]
            cos = jnp.cos(freqs).astype(x.dtype)
            sin = jnp.sin(freqs).astype(x.dtype)
            x1, x2 = (x[..., :D // 2], x[..., D // 2:])
            return jnp.concatenate([x1 * cos - x2 * sin, x2 * cos + x1 * sin], axis=-1)
        key = jax.random.key(seed)
        ks = jax.random.split(key, 5)
        s = 1.0 / np.sqrt(EMBED)
        return {'x': jax.random.normal(ks[0], (B, T, EMBED), dtype=jnp.float32), 'Wq': jax.random.normal(ks[1], (EMBED, EMBED), dtype=jnp.float32) * s, 'bq': jnp.zeros((EMBED,), dtype=jnp.float32), 'Wk': jax.random.normal(ks[2], (EMBED, EMBED), dtype=jnp.float32) * s, 'bk': jnp.zeros((EMBED,), dtype=jnp.float32), 'Wv': jax.random.normal(ks[3], (EMBED, EMBED), dtype=jnp.float32) * s, 'bv': jnp.zeros((EMBED,), dtype=jnp.float32), 'Wo': jax.random.normal(ks[4], (EMBED, EMBED), dtype=jnp.float32) * s, 'bo': jnp.zeros((EMBED,), dtype=jnp.float32)}
    _L0_attn_a_in = _L0_attn_a_setup()

    def _L0_attn_b_setup():
        import jax, jax.numpy as jnp
        import numpy as np
        HIDDEN = 128
        HEADS = 16
        HEAD = HIDDEN // HEADS

        def _ternary_weight(key, shape):
            g = jax.random.normal(key, shape, dtype=jnp.float32)
            return jnp.where(jnp.abs(g) < 0.6, 0.0, jnp.sign(g)).astype(jnp.float32)

        def _tlin(x, w, s, b):
            return jnp.einsum('bsh,oh->bso', x, w) * s + b
        key = jax.random.key(seed)
        ks = jax.random.split(key, 10)
        x = jax.random.normal(ks[0], (2, 256, HIDDEN), dtype=jnp.float32)
        d = {'x': x}
        names = ['q', 'k', 'v', 'o']
        for i, n in enumerate(names):
            d[f'w_{n}'] = _ternary_weight(ks[1 + i], (HIDDEN, HIDDEN))
            d[f's_{n}'] = jnp.float32(0.02)
            d[f'b_{n}'] = jax.random.normal(ks[5 + i], (HIDDEN,), dtype=jnp.float32) * 0.02
        return d
    _L0_attn_b_in = _L0_attn_b_setup()

    def _L0_ffn_setup():
        import jax, jax.numpy as jnp
        import numpy as np
        ALPHA = 1.0
        key = jax.random.key(seed)
        ks = jax.random.split(key, 7)
        B, S, IN, OUT = (8, 1024, 128, 128)
        RANK, DDIM, UDIM = (4, 100, 50)
        return {'hidden_states': jax.random.normal(ks[0], (B, S, IN), dtype=jnp.float32), 'W': jax.random.normal(ks[1], (OUT, IN), dtype=jnp.float32) * 0.02, 'b': jax.random.normal(ks[2], (OUT,), dtype=jnp.float32) * 0.02, 'lora_down': jax.random.normal(ks[3], (RANK, DDIM), dtype=jnp.float32) * 0.1, 'lora_up': jax.random.normal(ks[4], (UDIM, RANK), dtype=jnp.float32) * 0.1, 'down_aux': jax.random.normal(ks[5], (DDIM, IN), dtype=jnp.float32) * 0.03, 'up_aux': jax.random.normal(ks[6], (OUT, UDIM), dtype=jnp.float32) * 0.03}
    _L0_ffn_in = _L0_ffn_setup()
    _d = {'L0_attn_a_x': _L0_attn_a_in['x'], 'L0_attn_a_Wq': _L0_attn_a_in['Wq'], 'L0_attn_a_bq': _L0_attn_a_in['bq'], 'L0_attn_a_Wk': _L0_attn_a_in['Wk'], 'L0_attn_a_bk': _L0_attn_a_in['bk'], 'L0_attn_a_Wv': _L0_attn_a_in['Wv'], 'L0_attn_a_bv': _L0_attn_a_in['bv'], 'L0_attn_a_Wo': _L0_attn_a_in['Wo'], 'L0_attn_a_bo': _L0_attn_a_in['bo'], 'L0_attn_b_w_q': _L0_attn_b_in['w_q'], 'L0_attn_b_s_q': _L0_attn_b_in['s_q'], 'L0_attn_b_b_q': _L0_attn_b_in['b_q'], 'L0_attn_b_w_k': _L0_attn_b_in['w_k'], 'L0_attn_b_s_k': _L0_attn_b_in['s_k'], 'L0_attn_b_b_k': _L0_attn_b_in['b_k'], 'L0_attn_b_w_v': _L0_attn_b_in['w_v'], 'L0_attn_b_s_v': _L0_attn_b_in['s_v'], 'L0_attn_b_b_v': _L0_attn_b_in['b_v'], 'L0_attn_b_w_o': _L0_attn_b_in['w_o'], 'L0_attn_b_s_o': _L0_attn_b_in['s_o'], 'L0_attn_b_b_o': _L0_attn_b_in['b_o'], 'L0_ffn_W': _L0_ffn_in['W'], 'L0_ffn_b': _L0_ffn_in['b'], 'L0_ffn_lora_down': _L0_ffn_in['lora_down'], 'L0_ffn_lora_up': _L0_ffn_in['lora_up'], 'L0_ffn_down_aux': _L0_ffn_in['down_aux'], 'L0_ffn_up_aux': _L0_ffn_in['up_aux']}
    _x0 = _d['L0_attn_a_x']
    _d['L0_attn_a_x'] = jax.random.normal(jax.random.fold_in(jax.random.key(seed), 1), (32, 256, 128), dtype=_x0.dtype)
    del _x0
    return _d

def reference(L0_attn_a_x, L0_attn_a_Wq, L0_attn_a_bq, L0_attn_a_Wk, L0_attn_a_bk, L0_attn_a_Wv, L0_attn_a_bv, L0_attn_a_Wo, L0_attn_a_bo, L0_attn_b_w_q, L0_attn_b_s_q, L0_attn_b_b_q, L0_attn_b_w_k, L0_attn_b_s_k, L0_attn_b_b_k, L0_attn_b_w_v, L0_attn_b_s_v, L0_attn_b_b_v, L0_attn_b_w_o, L0_attn_b_s_o, L0_attn_b_b_o, L0_ffn_W, L0_ffn_b, L0_ffn_lora_down, L0_ffn_lora_up, L0_ffn_down_aux, L0_ffn_up_aux):

    def _L0_attn_a_ref(x, Wq, bq, Wk, bk, Wv, bv, Wo, bo):
        import jax, jax.numpy as jnp
        import numpy as np
        EMBED = 128
        HEADS = 16
        HEAD_DIM = EMBED // HEADS
        B, T = (2, 256)
        ROPE_THETA = 10000.0

        def _rope(x):
            D = x.shape[-1]
            inv_freq = 1.0 / ROPE_THETA ** (jnp.arange(0, D, 2, dtype=jnp.float32) / D)
            freqs = jnp.arange(x.shape[2], dtype=jnp.float32)[:, None] * inv_freq[None, :]
            cos = jnp.cos(freqs).astype(x.dtype)
            sin = jnp.sin(freqs).astype(x.dtype)
            x1, x2 = (x[..., :D // 2], x[..., D // 2:])
            return jnp.concatenate([x1 * cos - x2 * sin, x2 * cos + x1 * sin], axis=-1)
        Bb, Tt, C = x.shape
        H, D = (HEADS, HEAD_DIM)

        def proj(W, b):
            return (jnp.einsum('btc,oc->bto', x, W) + b).reshape(Bb, Tt, H, D).transpose(0, 2, 1, 3)
        q = _rope(proj(Wq, bq))
        k = _rope(proj(Wk, bk))
        v = proj(Wv, bv)
        scale = jnp.sqrt(jnp.asarray(D, dtype=x.dtype))
        scores = jnp.einsum('bhtd,bhsd->bhts', q, k) / scale
        attn = jax.nn.softmax(scores, axis=-1)
        out = jnp.einsum('bhts,bhsd->bhtd', attn, v)
        out = out.transpose(0, 2, 1, 3).reshape(Bb, Tt, C)
        return jnp.einsum('btc,oc->bto', out, Wo) + bo

    def _L0_attn_b_ref(x, w_q, s_q, b_q, w_k, s_k, b_k, w_v, s_v, b_v, w_o, s_o, b_o):
        import jax, jax.numpy as jnp
        import numpy as np
        HIDDEN = 128
        HEADS = 16
        HEAD = HIDDEN // HEADS

        def _ternary_weight(key, shape):
            g = jax.random.normal(key, shape, dtype=jnp.float32)
            return jnp.where(jnp.abs(g) < 0.6, 0.0, jnp.sign(g)).astype(jnp.float32)

        def _tlin(x, w, s, b):
            return jnp.einsum('bsh,oh->bso', x, w) * s + b
        B, S, H = x.shape

        def split_heads(t):
            return t.reshape(B, S, HEADS, HEAD).transpose(0, 2, 1, 3)
        q = split_heads(_tlin(x, w_q, s_q, b_q))
        k = split_heads(_tlin(x, w_k, s_k, b_k))
        v = split_heads(_tlin(x, w_v, s_v, b_v))
        scores = jnp.einsum('bhqd,bhkd->bhqk', q, k) / jnp.sqrt(jnp.float32(HEAD))
        attn = jax.nn.softmax(scores, axis=-1)
        ctx = jnp.einsum('bhqk,bhkd->bhqd', attn, v)
        ctx = ctx.transpose(0, 2, 1, 3).reshape(B, S, H)
        return _tlin(ctx, w_o, s_o, b_o)

    def _L0_ffn_ref(hidden_states, W, b, lora_down, lora_up, down_aux, up_aux):
        import jax, jax.numpy as jnp
        import numpy as np
        ALPHA = 1.0
        lilora_weight = up_aux @ (lora_up @ (lora_down @ down_aux))
        base = jnp.einsum('bsi,oi->bso', hidden_states, W) + b
        delta = jnp.einsum('bsi,oi->bso', hidden_states, lilora_weight)
        return base + ALPHA * delta
    x = L0_attn_a_x
    x = x + _L0_attn_a_ref(_layernorm(x, axis=-1), L0_attn_a_Wq, L0_attn_a_bq, L0_attn_a_Wk, L0_attn_a_bk, L0_attn_a_Wv, L0_attn_a_bv, L0_attn_a_Wo, L0_attn_a_bo)
    x = x + _L0_ffn_ref(_layernorm(x, axis=-1), L0_ffn_W, L0_ffn_b, L0_ffn_lora_down, L0_ffn_lora_up, L0_ffn_down_aux, L0_ffn_up_aux)
    x = x + _L0_attn_b_ref(_layernorm(x, axis=-1), L0_attn_b_w_q, L0_attn_b_s_q, L0_attn_b_b_q, L0_attn_b_w_k, L0_attn_b_s_k, L0_attn_b_b_k, L0_attn_b_w_v, L0_attn_b_s_v, L0_attn_b_b_v, L0_attn_b_w_o, L0_attn_b_s_o, L0_attn_b_b_o)
    x = x + _L0_ffn_ref(_layernorm(x, axis=-1), L0_ffn_W, L0_ffn_b, L0_ffn_lora_down, L0_ffn_lora_up, L0_ffn_down_aux, L0_ffn_up_aux)
    return x

_drawn_inputs = setup_inputs


def setup_inputs(seed=0):
    import zlib

    import numpy as np

    out = dict(_drawn_inputs(seed))
    spreads = {'L0_attn_a_bq': (0.0, 0.664),
     'L0_attn_a_bk': (0.0, 0.8),
     'L0_attn_a_bv': (0.0, 0.1),
     'L0_attn_a_bo': (0.0, 0.1)}
    factors = {'L0_attn_b_w_q': 8.0,
     'L0_attn_b_b_q': 8.0,
     'L0_attn_b_w_k': 8.0,
     'L0_attn_b_b_k': 8.0,
     'L0_attn_b_w_v': 8.0,
     'L0_attn_b_b_v': 8.0,
     'L0_attn_b_w_o': 8.0,
     'L0_attn_b_b_o': 2.891}
    for name, (base, spread) in spreads.items():
        noise = np.random.default_rng([zlib.crc32(name.encode()), seed]).standard_normal(out[name].shape)
        drawn = base * np.exp(spread * noise) if base else spread * noise
        out[name] = jnp.asarray(drawn.astype(out[name].dtype))
    for name, factor in factors.items():
        out[name] = (out[name] * factor).astype(out[name].dtype)
    return out
```

```python
import concourse.bass as bass
from concourse import mybir
from contextlib import ExitStack

TURNS, HALF = 64, 32
T, C, H, D = 256, 128, 16, 8
TT = T // 128
TERMS = [(0, 0), (0, 1), (0, 2), (1, 0), (1, 1), (2, 0)]
TERM_RUNS = [(0, 3), (1, 2), (2, 1)]
KMAX = 72
KALL = 74
SLOTS = H // 2
LN_EPS = 1e-5
FIRST, LAST = -5, TURNS + 2
UNROLL = 4
SEGMENTS = [(FIRST, 12, False), (7, 20, True), (27, 8, False), (35, 24, True), (59, 8, False)]


class Step:

    def __init__(self, c, i=None):
        self.c, self.i = c, i

    def has(self, off):
        return 0 <= self.c + off < TURNS

    def second(self, off):
        return self.c + off >= HALF

    def ring(self, off, size):
        return (self.c + off) % size

    def lin(self, per, off, extra=0):
        base = per * (self.c + off) + extra
        return base if self.i is None else self.i * (UNROLL * per) + base


def reach(eng, sem, n, per, off, extra=0):
    if per * (n.c + off) + extra > 0:
        eng.wait_ge(sem, n.lin(per, off, extra))


def reach_all(eng, n, *targets):
    values = [(sem, n.lin(per, off, extra)) for sem, per, off, extra in targets if per * (n.c + off) + extra > 0]
    if n.i is not None:
        values = [(sem, eng.to_reg(value)) for sem, value in values]
    for sem, value in values:
        eng.wait_ge(sem, value)


def steps(eng, body):
    for first, count, looped in SEGMENTS:
        if looped:
            with eng.Fori(0, count // UNROLL) as i:
                for u in range(UNROLL):
                    body(Step(first + u, i))
        else:
            for c in range(first, first + count):
                body(Step(c))


def build(nc, io, out):
    F32, BF16 = mybir.dt.float32, mybir.dt.bfloat16
    ALU, ACT, AX = mybir.AluOpType, mybir.ActivationFunctionType, mybir.AxisListType.X

    ctx = ExitStack()
    with ctx:
        def sb(name, shape, dt=F32):
            return ctx.enter_context(nc.sbuf_tensor(name, shape, dt))

        def sem(name):
            return ctx.enter_context(nc.semaphore(name))

        mid = nc.dram_tensor("mid", [HALF, T, C], F32, kind="Internal").ap()
        parts_dram = nc.dram_tensor("parts_dram", [2, 3, 2, 128, T], BF16, kind="Internal").ap()
        rsum_dram = nc.dram_tensor("rsum_dram", [128, 32], F32, kind="Internal").ap()

        ident = sb("ident", [128, 128])
        cos_t = sb("cos_t", [128, 2, T])
        sin_t = sb("sin_t", [128, 2, T])
        wqT = sb("wqT", [128, 2, 128])
        wkT = sb("wkT", [128, 2, 128])
        wvT = sb("wvT", [128, 2, 128])
        woT = sb("woT", [128, 2, 128])
        woP = sb("woP", [128, 2, 2, 128])
        wfT = sb("wfT", [128, 128])
        cols = sb("cols", [128, 2, 3])
        scal = sb("scal", [128, 4])
        bo_rows = sb("bo_rows", [128, 2, 128])
        bf_rows = sb("bf_rows", [128, 128])
        bv_rep = sb("bv_rep", [128, 2, 128])
        lo_downT = sb("lo_downT", [100, 4])
        aux_down = sb("aux_down", [100, 128])
        lo_upT = sb("lo_upT", [4, 50])
        aux_upT = sb("aux_upT", [50, 128])
        lo1 = sb("lo1", [4, 128])
        lo2 = sb("lo2", [50, 128])
        half_neg = sb("half_neg", [128, TT])

        xa = sb("xa", [128, 2, 2, TT, C])
        xr = sb("xr", [128, 2, 2, TT, C])
        x2 = sb("x2", [128, 2, 2, TT, C])
        xn = sb("xn", [128, TT, C])
        xnT = sb("xnT", [128, 4, T])
        qk_raw = sb("qk_raw", [128, 2, T])
        qk_swap = sb("qk_swap", [128, 2, T])
        qk_cos = sb("qk_cos", [128, 2, T])
        qk = sb("qk", [128, 2, T])
        rest = sb("rest", [128, 2, T])
        part = sb("part", [128, 3, 2, T], BF16)
        qs = sb("qs", [KALL + 22, 4, H, T], BF16)
        ks = sb("ks", [KALL + 22, 4, H, T], BF16)
        mx = sb("mx", [128, 2, TT, H])
        mrow = sb("mrow", [H, 2, 2, T], BF16)
        vpad = sb("vpad", [128, 2, TT, 2, 8, 32])
        pt = sb("pt", [128, 4, 4, TT, T])
        o_sb = sb("o_sb", [128, 2, 2, T])
        rs = sb("rs", [128, 32])
        rinv = sb("rinv", [128, 32])
        rb = sb("rb", [128, 2, T])
        ctxn = sb("ctxn", [128, 2, T])
        xb = sb("xb", [128, TT, C])
        x1 = sb("x1", [128, TT, C])
        x1b = sb("x1b", [128, TT, C])
        x1n = sb("x1n", [128, TT, C])
        x1nT = sb("x1nT", [128, T])
        st1 = sb("st1", [128, TT, 6])
        mv1 = sb("mv1", [128, TT, 2])
        ve1 = sb("ve1", [128, TT])
        rstd1 = sb("rstd1", [128, TT])
        st2 = sb("st2", [128, TT, 6])
        mv2 = sb("mv2", [128, TT, 2])
        ve2 = sb("ve2", [128, TT])
        rstd2 = sb("rstd2", [128, TT])

        ps_st = ctx.enter_context(nc.psum_tensor("ps_st", [128, 2, 2, TT, T], F32))
        ps_mx = ctx.enter_context(nc.psum_tensor("ps_mx", [128, 2, TT, T], F32))
        ps_pv = ctx.enter_context(nc.psum_tensor("ps_pv", [128, 2, T], F32))
        ps_m = ctx.enter_context(nc.psum_tensor("ps_m", [128, 512], F32))

        consts_in = sem("consts_in")
        setup_pe, setup_dve, setup_pool = sem("setup_pe"), sem("setup_dve"), sem("setup_pool")
        xa_in = sem("xa_in")
        xr_in = sem("xr_in")
        x2_out = sem("x2_out")
        parts_out = sem("parts_out")
        stacks_in = sem("stacks_in")
        mrows_in = sem("mrows_in")
        rsum_in = sem("rsum_in")
        rinv_out = sem("rinv_out")
        rb_in = sem("rb_in")
        aggr1, aggr2 = sem("aggr1"), sem("aggr2")
        stats1, ve1_ok, rstd1_ok, xn_ok = sem("stats1"), sem("ve1_ok"), sem("rstd1_ok"), sem("xn_ok")
        xnT_ps, xnT_ok = sem("xnT_ps"), sem("xnT_ok")
        qk_ps, qk_ok, rope_a, rope_ok = sem("qk_ps"), sem("qk_ok"), sem("rope_a"), sem("rope_ok")
        part1_ok, part2_ok, rest_ok, parts_ok = sem("part1_ok"), sem("part2_ok"), sem("rest_ok"), sem("parts_ok")
        v_ps, v_ok = sem("v_ps"), sem("v_ok")
        mx_ps = sem("mx_ps")
        mx_ok = sem("mx_ok")
        mrow_ps, mrow1_ok, mrow2_ok = sem("mrow_ps"), sem("mrow1_ok"), sem("mrow2_ok")
        st_ps = sem("st_ps")
        exp_ok = sem("exp_ok")
        pv_ps = sem("pv_ps")
        o_ok, rinv_ok, norm_ok = sem("o_ok"), sem("rinv_ok"), sem("norm_ok")
        y_ps, xb_ok, x1_ok, x1b_ok = sem("y_ps"), sem("xb_ok"), sem("x1_ok"), sem("x1b_ok")
        stats2, ve2_ok, rstd2_ok, x1n_ok = sem("stats2"), sem("ve2_ok"), sem("rstd2_ok"), sem("x1n_ok")
        x1nT_ps, x1nT_ok = sem("x1nT_ps"), sem("x1nT_ok")
        z_ps, x2_ok = sem("z_ps"), sem("x2_ok")

        block = ctx.enter_context(nc.Block())

        loads = [(ident[:, :], io["ident"]), (cos_t[:, :, :], io["cos_t"]), (sin_t[:, :, :], io["sin_t"]),
                 (wfT[:, :], io["wfT"]), (lo_downT[:, :], io["lo_downT"]), (aux_down[:, :], io["aux_down"]),
                 (lo_upT[:, :], io["lo_upT"]), (aux_upT[:, :], io["aux_upT"]),
                 (bf_rows[:, :], io["bf"].partition_broadcast(128))]
        for a in range(2):
            loads += [(w[:, a, :], io[f"{n}{a}"]) for w, n in ((wqT, "wqT"), (wkT, "wkT"), (wvT, "wvT"), (woT, "woT"))]
            loads += [(woP[:, a, :, :], io[f"woP{a}"].rearrange("r p o -> p r o")),
                      (cols[:, a, :], io[f"cols{a}"]), (bo_rows[:, a, :], io[f"bo{a}"].partition_broadcast(128))]
        loads += [(scal[:, :], io["scal"].partition_broadcast(128))]
        N_CONST = 16 * len(loads)
        N_FIXED = 14

        def pair_of(tensor, n, off):
            view = tensor.rearrange("(g two) (i p) c -> p g two i c", two=2, p=128)
            base = (n.c + off) // 2 % (HALF // 2)
            if n.i is None:
                return view[:, base]
            return view[:, bass.ds(n.i * (UNROLL // 2) + base, 1)].rearrange("p g two i c -> p (g two) i c")

        @block.sync
        def _(sp):
            for dst, src in loads:
                sp.dma_start(dst, src).then_inc(consts_in, 16)
            sp.wait_ge(setup_pool, N_FIXED)

            def step(n):
                load_xa, load_xr = n.c % 2 and n.has(5), n.c % 2 and n.has(-1)
                store = n.c % 2 == 0 and n.has(-3)
                if n.has(3):
                    reach_all(sp, n,
                              (stacks_in, 96, 3, 0),
                              (parts_out, 16, 4, 0),
                              (st_ps, 8, 0, 0))
                    src = parts_dram[n.ring(3, 2)].rearrange("s w (d h) t -> s w d (h t)", d=D)
                    row = 0
                    for a, many in TERM_RUNS:
                        q_src = src[a:a + 1, 0].broadcast_to((many, D, H * T))
                        sp.dma_start(qs[row:row + many * D, n.ring(3, 4)], q_src).then_inc(stacks_in, 16)
                        sp.dma_start(ks[row:row + many * D, n.ring(3, 4)], src[0:many, 1]).then_inc(stacks_in, 16)
                        row += many * D
                waits = []
                if n.has(1):
                    waits += [(mrows_in, 32, 1, 0), (mrow1_ok, 1, 2, 0), (mrow2_ok, 1, 2, 0)]
                if load_xa:
                    waits += [(xa_in, 8, 5, 0), (xn_ok, 1, 3, 0)]
                    if n.second(5):
                        waits += [(x2_out, 8, 7 - HALF, 0)]
                if load_xr:
                    waits += [(xr_in, 8, -1, 0), (xb_ok, 1, -3, 0)]
                reach_all(sp, n, *waits)
                if n.has(1):
                    for i in range(2):
                        sp.dma_start(qs[KMAX + i:KMAX + i + 1, n.ring(1, 4)], mrow[:, n.ring(1, 2), i]
                                     ).then_inc(mrows_in, 16)
                if load_xa:
                    sp.dma_start(xa[:, (n.c + 5) // 2 % 2], pair_of(mid if n.second(5) else io["x"], n, 5)
                                 ).then_inc(xa_in, 16)
                if load_xr:
                    sp.dma_start(xr[:, (n.c - 1) // 2 % 2], pair_of(mid if n.second(-1) else io["x"], n, -1)
                                 ).then_inc(xr_in, 16)
                waits = []
                if n.has(-1):
                    waits += [(rsum_in, 32, -1, 0), (o_ok, 1, 0, 0), (rinv_ok, 1, -1, 0)]
                if store:
                    waits += [(x2_out, 8, -4, 0), (x2_ok, 1, -2, 0)]
                reach_all(sp, n, *waits)
                if n.has(-1):
                    for i in range(2):
                        sp.dma_start(rs[64 * i:64 * i + 64, :], o_sb[16 + i:128:32, n.ring(-1, 2)]
                                     ).then_inc(rsum_in, 16)
                if store:
                    sp.dma_start(pair_of(out if n.second(-3) else mid, n, -4), x2[:, (n.c - 4) // 2 % 2]
                                 ).then_inc(x2_out, 16)
                if n.has(-1):
                    reach_all(sp, n, (rinv_ok, 1, 0, 0), (rb_in, 32, -1, 0))
                    sp.dma_start(rsum_dram, rinv[:, :]).then_inc(rinv_out, 16)
                    reach_all(sp, n, (rinv_out, 16, 0, 0), (norm_ok, 1, -1, 0))
                    back = rsum_dram.rearrange("(i j c) n -> i j (c n)", i=2, j=4)
                    for i in range(2):
                        sp.dma_start(rb[i:128:2], back[i].unsqueeze(1).broadcast_to((4, 16, 512))
                                     ).then_inc(rb_in, 16)
                if n.has(4):
                    reach_all(sp, n, (parts_ok, 1, 5, 0), (stacks_in, 96, 3, 0))
                    sp.dma_start(parts_dram[n.ring(4, 2)].rearrange("s w p t -> p (s w) t"),
                                 part[:, :, :, :].rearrange("p s w t -> p (s w) t")).then_inc(parts_out, 16)
            steps(sp, step)
            sp.wait_ge(x2_out, 8 * TURNS)

        @block.gpsimd
        def _(pool):
            fixed = [(half_neg[:, :], -0.5)]
            for p in (32, 64):
                fixed += [(qs[p:p + 32], 0.0), (ks[p:p + 32], 1.0)]
            fixed += [(vpad[:, :, :, :, :, :], 0.0)]
            fixed += [(vpad[:, ring, s, i, :, 16 + i:32:2], 1.0)
                      for i in range(2) for ring in range(2) for s in range(TT)]
            assert len(fixed) == N_FIXED
            for done, (place, value) in enumerate(fixed):
                nc.gpsimd.memset(place, value).then_inc(setup_pool, 1)
                pool.wait_ge(setup_pool, done + 1)
            pool.wait_ge(setup_dve, 5)

            def step(n):
                if n.has(-2):
                    reach(pool, rb_in, n, 32, -1)
                    reach(pool, y_ps, n, 1, -2)
                    nc.gpsimd.tensor_tensor(ctxn[:, :, :], o_sb[:, n.ring(-2, 2)], rb[:, :, :], ALU.mult
                                            ).then_inc(norm_ok, 1)
                    if n.c % 2 == 0:
                        reach(pool, xr_in, n, 8, 0)
                    reach(pool, x1_ok, n, 1, -2)
                    bias = bo_rows[:, int(n.second(-2)), :].unsqueeze(1).broadcast_to((128, TT, C))
                    nc.gpsimd.tensor_tensor(xb[:, :, :], xr[:, (n.c - 2) // 2 % 2, n.c % 2], bias, ALU.add
                                            ).then_inc(xb_ok, 1)
                rope = n.has(4) and not n.second(4)
                if rope:
                    reach(pool, qk_ok, n, 1, 5)
                    nc.gpsimd.tensor_tensor(qk_cos[:, :, :], qk_raw[:, :, :], cos_t[:, :, :], ALU.mult)
                    nc.gpsimd.tensor_tensor(qk_swap[:, :, :], qk_swap[:, :, :], sin_t[:, :, :], ALU.mult
                                            ).then_inc(rope_a, 1)
                if n.has(-2):
                    reach(pool, ve2_ok, n, 1, -1)
                    nc.gpsimd.tensor_tensor(rstd2[:, :], ve2[:, :], half_neg[:, :], ALU.pow).then_inc(rstd2_ok, 1)
                if rope:
                    reach(pool, rope_a, n, 1, 5)
                    reach(pool, parts_ok, n, 1, 4)
                    nc.gpsimd.tensor_tensor(qk[:, :, :], qk_cos[:, :, :], qk_swap[:, :, :], ALU.add
                                            ).then_inc(rope_ok, 1)
                if n.has(-2):
                    reach(pool, x1_ok, n, 1, -1)
                    reach(pool, x2_ok, n, 1, -2)
                    nc.gpsimd.tensor_tensor(x1b[:, :, :], x1[:, :, :],
                                            bf_rows[:, :].unsqueeze(1).broadcast_to((128, TT, C)), ALU.add
                                            ).then_inc(x1b_ok, 1)
                if n.has(5):
                    reach(pool, ve1_ok, n, 1, 6)
                    nc.gpsimd.tensor_tensor(rstd1[:, :], ve1[:, :], half_neg[:, :], ALU.pow).then_inc(rstd1_ok, 1)
                if n.has(4):
                    reach(pool, part1_ok, n, 1, 5)
                    nc.gpsimd.tensor_tensor(part[:, 1], qk[:, :, :], part[:, 0], ALU.subtract)
                    nc.gpsimd.tensor_tensor(rest[:, :, :], qk[:, :, :], part[:, 0], ALU.subtract).then_inc(rest_ok, 1)
                    reach(pool, rest_ok, n, 1, 5)
                    nc.gpsimd.tensor_tensor(part[:, 2], rest[:, :, :], part[:, 1], ALU.subtract).then_inc(parts_ok, 1)
            steps(pool, step)

        @block.scalar
        def _(act):
            act.wait_ge(consts_in, N_CONST)
            act.wait_ge(setup_pool, N_FIXED)
            act.wait_ge(setup_dve, 5)

            def step(n):
                for k in range(SLOTS):
                    if n.has(0):
                        u = k // 2
                        act.wait_ge(st_ps, n.lin(8, 0, k + 1))
                        if k % 2 == 0:
                            reach(act, pv_ps, n, 4, -1, u + 1)
                        nc.scalar.activation(pt[:, u, 2 * (k % 2):2 * (k % 2) + 2], ps_st[:, k % 2], ACT.Exp,
                                             scale=float(D) ** -0.5).then_inc(exp_ok, 1)
                    if k == 1 and n.has(4):
                        reach(act, xnT_ps, n, 1, 5)
                        reach(act, v_ps, n, 1, 1)
                        nc.scalar.activation(xnT[:, n.ring(4, 4)], ps_m[:, 0:T], ACT.Copy).then_inc(xnT_ok, 1)
                    if k == 2 and n.has(1):
                        reach(act, mrow_ps, n, 1, 2)
                        reach(act, mrows_in, n, 32, 0)
                        nc.scalar.activation(mrow[:, n.ring(1, 2), 0], ps_m[0:H, 0:T], ACT.Copy).then_inc(mrow1_ok, 1)
                    if k == 2 and n.has(-1):
                        reach(act, pv_ps, n, 4, 0)
                        reach(act, norm_ok, n, 1, -2)
                        nc.scalar.activation(o_sb[:, n.ring(-1, 2)], ps_pv[:, :, :], ACT.Copy).then_inc(o_ok, 1)
                    if k == 3 and n.has(4):
                        reach(act, qk_ps, n, 1, 5)
                        if n.second(4):
                            reach(act, parts_ok, n, 1, 4)
                            for w in range(2):
                                last = nc.scalar.activation(qk[:, w], ps_m[:, w * T:(w + 1) * T], ACT.Identity,
                                                            scale=scal[:, w:w + 1], bias=cols[:, 1, w:w + 1])
                        else:
                            reach(act, rope_ok, n, 1, 4)
                            for w in range(2):
                                src = ps_m[:, w * T:(w + 1) * T]
                                nc.scalar.activation(qk_raw[:, w], src, ACT.Identity, bias=cols[:, 0, w:w + 1])
                                nc.scalar.activation(qk_swap[0:64, w], src[64:128], ACT.Identity,
                                                     bias=cols[64:128, 0, w:w + 1])
                                last = nc.scalar.activation(qk_swap[64:128, w], src[0:64], ACT.Identity,
                                                            bias=cols[0:64, 0, w:w + 1])
                        last.then_inc(qk_ok, 1)
                    if k == 5 and n.has(1):
                        reach(act, v_ps, n, 1, 2)
                        reach(act, pv_ps, n, 4, 0)
                        scale = scal[:, 2:3] if n.second(1) else 1.0
                        src = ps_m[:, 0:TT * C].rearrange("p (s i h d) -> p s i h d", s=TT, i=2, h=8)
                        for i in range(2):
                            last = nc.scalar.activation(vpad[:, n.ring(1, 2), :, i, :, i:16:2], src[:, :, i],
                                                        ACT.Identity, scale=scale)
                        last.then_inc(v_ok, 1)
                    if k == 7 and n.has(-2):
                        reach(act, x1nT_ps, n, 1, -1)
                        reach(act, z_ps, n, 1, -2)
                        nc.scalar.activation(x1nT[:, :], ps_m[:, 0:T], ACT.Copy).then_inc(x1nT_ok, 1)
            steps(act, step)

        @block.vector
        def _(dve):
            dve.wait_ge(consts_in, N_CONST)
            dve.wait_ge(setup_pe, 1)
            nc.vector.tensor_copy(lo1[:, :], ps_m[0:4, 0:128]).then_inc(setup_dve, 1)
            for a in range(2):
                nc.vector.tensor_copy(bv_rep[:, a], cols[:, a, 2:3].broadcast_to((128, 128)))
            dve.wait_ge(setup_pe, 2)
            nc.vector.tensor_copy(lo2[:, :], ps_m[0:50, 0:128]).then_inc(setup_dve, 1)
            dve.wait_ge(setup_pe, 3)
            nc.vector.tensor_tensor(wfT[:, :], ps_m[:, 0:128], wfT[:, :], ALU.add).then_inc(setup_dve, 1)
            dve.wait_ge(setup_pe, 4)
            nc.vector.tensor_tensor(bo_rows[:, 0], ps_m[:, 0:128], bo_rows[:, 0], ALU.add).then_inc(setup_dve, 1)
            nc.vector.scalar_tensor_tensor(bo_rows[:, 1], ps_m[:, 128:256], scal[:, 3:4], bo_rows[:, 1],
                                           ALU.mult, ALU.add).then_inc(setup_dve, 1)

            def statistics(x, stat, done):
                for i in range(TT):
                    last = nc.vector.bn_stats(stat[:, i, :], x[:, i, :])
                last.then_inc(done, 1)

            def variance(stat, mv, ve, n, off, stats_sem, aggr_sem, ve_sem):
                for i in range(TT):
                    last = nc.vector.bn_aggr(mv[:, i, :], stat[:, i, :])
                last.then_inc(aggr_sem, 1)
                reach(dve, aggr_sem, n, 1, off, 1)
                nc.vector.tensor_scalar(ve[:, :], mv[:, :, 1], LN_EPS, None, ALU.add).then_inc(ve_sem, 1)

            def step(n):
                xa_now = xa[:, (n.c + 5) // 2 % 2, (n.c + 5) % 2]
                for k in range(SLOTS):
                    if k == 0 and n.has(2):
                        reach(dve, mrow_ps, n, 1, 1)
                    for b in range(2):
                        if b == 1 and k == 5 and n.has(-2):
                            reach(dve, stats2, n, 1, -1)
                        if b == 1 and k == 6 and n.has(5):
                            reach(dve, stats1, n, 1, 6)
                        if n.has(2):
                            dve.wait_ge(mx_ps, n.lin(16, 2, 2 * k + b + 1))
                            nc.vector.tensor_reduce(mx[:, n.ring(2, 2), :, 2 * k + b], ps_mx[:, b], AX, ALU.max,
                                                    negate=True).then_inc(mx_ok, 1)
                    if k == 0 and n.has(-3):
                        reach(dve, z_ps, n, 1, -2)
                        reach(dve, x1b_ok, n, 1, -2)
                        if n.c % 2:
                            reach(dve, x2_out, n, 8, -7)
                        nc.vector.tensor_tensor(x2[:, (n.c - 3) // 2 % 2, (n.c - 3) % 2],
                                                ps_m[:, 0:TT * C].rearrange("p (i c) -> p i c", i=TT), x1b[:, :, :],
                                                ALU.add).then_inc(x2_ok, 1)
                    if k == 2 and n.has(1):
                        reach(dve, mrow1_ok, n, 1, 2)
                        nc.vector.tensor_tensor(mrow[:, n.ring(1, 2), 1], ps_m[0:H, 0:T], mrow[:, n.ring(1, 2), 0],
                                                ALU.subtract).then_inc(mrow2_ok, 1)
                    if k == 4 and n.has(-2):
                        reach(dve, y_ps, n, 1, -1)
                        reach(dve, xb_ok, n, 1, -1)
                        reach(dve, x1b_ok, n, 1, -2)
                        y = ps_m[:, 0:TT * C].rearrange("p (i c) -> p i c", i=TT)
                        if n.second(-2):
                            nc.vector.scalar_tensor_tensor(x1[:, :, :], y, scal[:, 3:4], xb[:, :, :],
                                                           ALU.mult, ALU.add).then_inc(x1_ok, 1)
                        else:
                            nc.vector.tensor_tensor(x1[:, :, :], y, xb[:, :, :], ALU.add).then_inc(x1_ok, 1)
                        reach(dve, x1_ok, n, 1, -1)
                        statistics(x1, st2, stats2)
                    if k == 5 and n.has(-2):
                        variance(st2, mv2, ve2, n, -2, stats2, aggr2, ve2_ok)
                    if k == 5 and n.has(-1):
                        reach(dve, rsum_in, n, 32, 0)
                        reach(dve, rinv_out, n, 16, -1)
                        nc.vector.reciprocal(rinv[:, :], rs[:, :]).then_inc(rinv_ok, 1)
                    if k == 5 and n.has(5):
                        if n.c % 2:
                            reach(dve, xa_in, n, 8, 7)
                        statistics(xa_now, st1, stats1)
                    if k == 6 and n.has(5):
                        variance(st1, mv1, ve1, n, 5, stats1, aggr1, ve1_ok)
                    if k == 6 and n.has(-2):
                        reach(dve, rstd2_ok, n, 1, -1)
                        reach(dve, x1nT_ps, n, 1, -2)
                        for i in range(TT):
                            last = nc.vector.tensor_scalar(x1n[:, i], x1[:, i], mv2[:, i, 0:1], rstd2[:, i:i + 1],
                                                           ALU.subtract, ALU.mult)
                        last.then_inc(x1n_ok, 1)
                if n.has(5):
                    reach(dve, rstd1_ok, n, 1, 6)
                    reach(dve, xnT_ps, n, 1, 5)
                    for i in range(TT):
                        last = nc.vector.tensor_scalar(xn[:, i], xa_now[:, i], mv1[:, i, 0:1], rstd1[:, i:i + 1],
                                                       ALU.subtract, ALU.mult)
                    last.then_inc(xn_ok, 1)
                if n.has(4):
                    if n.second(4):
                        reach(dve, qk_ok, n, 1, 5)
                    else:
                        reach(dve, rope_ok, n, 1, 5)
                    reach(dve, parts_out, n, 16, 4)
                    nc.vector.tensor_copy(part[:, 0], qk[:, :, :]).then_inc(part1_ok, 1)
            steps(dve, step)

        @block.tensor
        def _(pe):
            mm = nc.tensor.matmul
            pe.wait_ge(consts_in, N_CONST)
            mm(ps_m[0:4, 0:128], lo_downT[:, :], aux_down[:, :], start=True, stop=True).then_inc(setup_pe, 1)
            pe.wait_ge(setup_dve, 1)
            mm(ps_m[0:50, 0:128], lo_upT[:, :], lo1[:, :], start=True, stop=True).then_inc(setup_pe, 1)
            pe.wait_ge(setup_dve, 2)
            mm(ps_m[:, 0:128], lo2[:, :], aux_upT[:, :], start=True, stop=True).then_inc(setup_pe, 1)
            pe.wait_ge(setup_dve, 3)
            for a in range(2):
                last = mm(ps_m[:, a * 128:a * 128 + 128], bv_rep[:, a], woT[:, a], start=True, stop=True)
            last.then_inc(setup_pe, 1)
            pe.wait_ge(setup_dve, 5)
            pe.wait_ge(setup_pool, N_FIXED)

            def key_major_scores(n, k):
                if k == 0:
                    reach(pe, mrows_in, n, 32, 1)
                reach(pe, exp_ok, n, 8, 0, k - 1)
                r = n.ring(0, 4)
                for b in range(2):
                    for s in range(TT):
                        last = mm(ps_st[:, k % 2, b, s], ks[0:KALL, r, 2 * k + b, s * 128:s * 128 + 128],
                                  qs[0:KALL, r, 2 * k + b, :], start=True, stop=True)
                last.then_inc(st_ps, 1)

            def token_major_scores(n, k):
                if k == 0:
                    reach(pe, stacks_in, n, 96, 3)
                r = n.ring(2, 4)
                for b in range(2):
                    reach(pe, mx_ok, n, 16, 2, 2 * k + b - 1)
                    for i in range(TT):
                        last = mm(ps_mx[:, b, i], qs[0:KMAX, r, 2 * k + b, i * 128:i * 128 + 128],
                                  ks[0:KMAX, r, 2 * k + b, :], start=True, stop=True)
                    last.then_inc(mx_ps, 1)

            def times_v(n, off, u, s):
                i, r = u % 2, u // 2
                if s == 0:
                    reach(pe, exp_ok, n, 8, off, 2 * u + 2)
                    if u == 0:
                        reach(pe, v_ok, n, 1, off + 1)
                        reach(pe, o_ok, n, 1, off)
                for j in range(4):
                    last = mm(ps_pv[32 * j:32 * j + 32, r], vpad[:, n.ring(off, 2), s, i, r * 4 + j, :],
                              pt[:, u, j, s], start=(i == 0 and s == 0), stop=(i == 1 and s == 1))
                if s == 1:
                    last.then_inc(pv_ps, 1)

            def small_product(n, k):
                if k == 0 and n.has(-3):
                    reach(pe, x1nT_ok, n, 1, -2)
                    for i in range(TT):
                        last = mm(ps_m[:, i * C:i * C + C], x1nT[:, i * 128:i * 128 + 128], wfT[:, :],
                                  start=True, stop=True)
                    last.then_inc(z_ps, 1)
                if k == 1 and n.has(4):
                    reach(pe, xn_ok, n, 1, 5)
                    if n.has(-3):
                        reach(pe, x2_ok, n, 1, -2)
                    elif n.has(0):
                        reach(pe, v_ok, n, 1, 1)
                    else:
                        reach(pe, qk_ok, n, 1, 4)
                    for i in range(TT):
                        last = nc.tensor.transpose(ps_m[:, i * 128:i * 128 + 128], xn[:, i], ident[:, :])
                    last.then_inc(xnT_ps, 1)
                if k == 2 and n.has(1):
                    reach(pe, mx_ok, n, 16, 2)
                    if n.has(4):
                        reach(pe, xnT_ok, n, 1, 5)
                    else:
                        reach(pe, x2_ok, n, 1, -2)
                    for i in range(TT):
                        last = mm(ps_m[0:H, i * 128:i * 128 + 128], mx[:, n.ring(1, 2), i, :], ident[:, :],
                                  start=True, stop=True)
                    last.then_inc(mrow_ps, 1)
                if k == 3 and n.has(4):
                    a = int(n.second(4))
                    reach(pe, xnT_ok, n, 1, 5)
                    if n.has(1):
                        reach(pe, mrow2_ok, n, 1, 2)
                    for w, weight in enumerate((wqT, wkT)):
                        last = mm(ps_m[:, w * T:(w + 1) * T], weight[:, a], xnT[:, n.ring(4, 4)],
                                  start=True, stop=True)
                    last.then_inc(qk_ps, 1)
                if k == 4 and n.has(-2):
                    a = int(n.second(-2))
                    reach(pe, norm_ok, n, 1, -1)
                    if n.has(4):
                        reach(pe, qk_ok, n, 1, 5)
                    elif n.has(1):
                        reach(pe, mrow2_ok, n, 1, 2)
                    elif n.has(-3):
                        reach(pe, x2_ok, n, 1, -2)
                    for i in range(TT):
                        for r in range(2):
                            last = mm(ps_m[:, i * C:i * C + C], ctxn[:, r, i * 128:i * 128 + 128], woP[:, a, r],
                                      start=(r == 0), stop=(r == 1))
                    last.then_inc(y_ps, 1)
                if k == 5 and n.has(1):
                    a = int(n.second(1))
                    if n.has(-2):
                        reach(pe, x1_ok, n, 1, -1)
                    elif n.has(4):
                        reach(pe, qk_ok, n, 1, 5)
                    for i in range(TT):
                        last = mm(ps_m[:, i * C:i * C + C], xnT[:, n.ring(1, 4), i * 128:i * 128 + 128], wvT[:, a],
                                  start=True, stop=True)
                    last.then_inc(v_ps, 1)
                if k == 7 and n.has(-2):
                    reach(pe, x1n_ok, n, 1, -1)
                    if n.has(1):
                        reach(pe, v_ok, n, 1, 2)
                    for i in range(TT):
                        last = nc.tensor.transpose(ps_m[:, i * 128:i * 128 + 128], x1n[:, i], ident[:, :])
                    last.then_inc(x1nT_ps, 1)

            def step(n):
                for k in range(SLOTS):
                    if n.has(0):
                        key_major_scores(n, k)
                    small_product(n, k)
                    if n.has(2):
                        token_major_scores(n, k)
                    if k >= 2 and n.has(0):
                        times_v(n, 0, (k - 2) // 2, k % 2)
                    if k < 2 and n.has(-1):
                        times_v(n, -1, 3, k)
            steps(pe, step)


def kernel(**inputs):
    import numpy as np
    import concourse.bacc as bacc
    from concourse.bass_utils import run_bass_kernel_spmd

    g = {k: np.asarray(v) for k, v in inputs.items()}
    a, b, f = "L0_attn_a_", "L0_attn_b_", "L0_ffn_"
    names = [(a + "Wq", a + "Wk", a + "Wv", a + "Wo", a + "bq", a + "bk", a + "bv", a + "bo"),
             (b + "w_q", b + "w_k", b + "w_v", b + "w_o", b + "b_q", b + "b_k", b + "b_v", b + "b_o")]
    qk_order = np.array([8 * h + d for d in range(8) for h in range(16)])
    head = lambda i, r, j: 4 * (2 * r + i) + j
    v_order = np.array([8 * head(i, r, j) + d for i in range(2) for r in range(2) for j in range(4) for d in range(8)])
    inv_freq = (1.0 / 10000.0 ** (np.arange(0, 8, 2, dtype=np.float32) / 8)).astype(np.float32)
    angle = np.arange(256, dtype=np.float32)[None, :] * inv_freq[:, None]
    cos_t = np.repeat(np.cos(angle), 16, axis=0)
    sin_t = np.repeat(np.sin(angle), 16, axis=0)
    cos_t = np.concatenate([cos_t, cos_t]).astype(np.float32)
    sin_t = np.concatenate([-sin_t, sin_t]).astype(np.float32)
    arrays = {
        "x": g[a + "x"], "ident": np.eye(128, dtype=np.float32),
        "cos_t": np.stack([cos_t, cos_t], axis=1), "sin_t": np.stack([sin_t, sin_t], axis=1),
        "wfT": g[f + "W"].T, "bf": g[f + "b"], "lo_downT": g[f + "lora_down"].T, "aux_down": g[f + "down_aux"],
        "lo_upT": g[f + "lora_up"].T, "aux_upT": g[f + "up_aux"].T,
        "scal": np.stack([g[b + "s_q"], g[b + "s_k"], g[b + "s_v"], g[b + "s_o"]]).reshape(4),
    }
    for n, (wq, wk, wv, wo, bq, bk, bv, bo) in enumerate(names):
        arrays[f"wqT{n}"] = g[wq][qk_order].T
        arrays[f"wkT{n}"] = g[wk][qk_order].T
        arrays[f"wvT{n}"] = g[wv][v_order].T
        arrays[f"woT{n}"] = g[wo].T
        padded = np.zeros((2, 128, 128), np.float32)
        for i in range(2):
            for r in range(2):
                for j in range(4):
                    padded[r, 32 * j + i:32 * j + 16:2] = g[wo].T[8 * head(i, r, j):8 * head(i, r, j) + 8]
        arrays[f"woP{n}"] = padded
        arrays[f"cols{n}"] = np.stack([g[bq][qk_order], g[bk][qk_order], g[bv]], axis=1)
        arrays[f"bo{n}"] = g[bo]
    arrays = {f"in_{k}": np.ascontiguousarray(v) for k, v in arrays.items()}

    nc = bacc.Bacc("TRN2", target_bir_lowering=False, num_devices=1)
    io = {k[3:]: nc.dram_tensor(k, v.shape, mybir.dt.from_np(v.dtype), kind="ExternalInput").ap()
          for k, v in arrays.items()}
    out = nc.dram_tensor("out", (32, 256, 128), mybir.dt.float32, kind="ExternalOutput").ap()
    build(nc, io, out)
    r = run_bass_kernel_spmd(nc, [arrays], core_ids=[0])
    return r.results[0]["out"]
```

```python
import concourse.bass as bass
from concourse import mybir
from contextlib import ExitStack

TURNS, HALF = 64, 32
T, C, H, D = 256, 128, 16, 8
TT = T // 128
TERMS = [(0, 0), (0, 1), (0, 2), (1, 0), (1, 1), (2, 0)]
TERM_RUNS = [(0, 3), (1, 2), (2, 1)]
KMAX = 72
KALL = 74
SLOTS = H // 2
LN_EPS = 1e-5
FIRST, LAST = -5, TURNS + 3
UNROLL = 4
SEGMENTS = [(FIRST, 11, False), (6, 20, True), (26, 11, False), (37, 20, True), (57, 11, False)]
assert SEGMENTS[-1][0] + SEGMENTS[-1][1] - 1 == LAST


ST_BANK = [0, 1, 2] * 5 + [1]
ST_BEFORE = [max(j for j in range(-H, h) if ST_BANK[j % H] == ST_BANK[h]) for h in range(H)]


class Step:

    def __init__(self, c, i=None):
        self.c, self.i = c, i

    def has(self, off):
        return 0 <= self.c + off < TURNS

    def second(self, off):
        return self.c + off >= HALF

    def ring(self, off, size):
        return (self.c + off) % size

    def lin(self, per, off, extra=0):
        base = per * (self.c + off) + extra
        return base if self.i is None else self.i * (UNROLL * per) + base


def reach(eng, sem, n, per, off, extra=0):
    if per * (n.c + off) + extra > 0:
        eng.wait_ge(sem, n.lin(per, off, extra))


def reach_all(eng, n, *targets):
    values = [(sem, n.lin(per, off, extra)) for sem, per, off, extra in targets if per * (n.c + off) + extra > 0]
    if n.i is not None:
        values = [(sem, eng.to_reg(value)) for sem, value in values]
    for sem, value in values:
        eng.wait_ge(sem, value)


def steps(eng, body):
    for first, count, looped in SEGMENTS:
        if looped:
            with eng.Fori(0, count // UNROLL) as i:
                for u in range(UNROLL):
                    body(Step(first + u, i))
        else:
            for c in range(first, first + count):
                body(Step(c))


PACKS = {
    "pack_first": [("ident", 128, 128), ("wqT0", 128, 128), ("wkT0", 128, 128), ("cols0", 128, 3), ("cols1", 128, 3),
                   ("lo_downT", 100, 4), ("aux_down", 100, 128), ("lo_upT", 4, 50), ("aux_upT", 50, 128),
                   ("wfT", 128, 128)],
    "pack_second": [("cos_t", 128, 512), ("sin_t", 128, 512), ("wqT1", 128, 128), ("wkT1", 128, 128)]
                   + [(f"{w}{a}{r}", 128, 128) for a in range(2)
                      for w, r in (("wvT", ""), ("woT", ""), ("woP", 0), ("woP", 1))],
    "pack_rows": [("bo0", 128, 128), ("bo1", 128, 128), ("bf", 128, 128), ("scal", 128, 4)],
}


def build(nc, io, out):
    F32, BF16 = mybir.dt.float32, mybir.dt.bfloat16
    ALU, ACT, AX = mybir.AluOpType, mybir.ActivationFunctionType, mybir.AxisListType.X

    ctx = ExitStack()
    with ctx:
        def sb(name, shape, dt=F32):
            return ctx.enter_context(nc.sbuf_tensor(name, shape, dt))

        def sem(name):
            return ctx.enter_context(nc.semaphore(name))

        mid = nc.dram_tensor("mid", [HALF, T, C], F32, kind="Internal").ap()
        parts_dram = nc.dram_tensor("parts_dram", [2, 3, 2, 128, T], BF16, kind="Internal").ap()
        rsum_dram = nc.dram_tensor("rsum_dram", [128, 32], F32, kind="Internal").ap()

        packed = {}
        for name, fields in PACKS.items():
            tile = sb(name, [128, sum(width for _, _, width in fields)])
            at = 0
            for field, rows, width in fields:
                packed[field] = tile[0:rows, at:at + width]
                at += width
            packed[name] = tile[:, :]
        ident, wfT = packed["ident"], packed["wfT"]
        cos_t, sin_t = (packed[f].rearrange("p (w t) -> p w t", w=2) for f in ("cos_t", "sin_t"))
        wqT, wkT, wvT, woT, cols, bo_rows = ([packed[f"{f}{a}"] for a in range(2)]
                                             for f in ("wqT", "wkT", "wvT", "woT", "cols", "bo"))
        woP = [[packed[f"woP{a}{r}"] for r in range(2)] for a in range(2)]
        bf_rows, scal = packed["bf"], packed["scal"]
        lo_downT, aux_down, lo_upT, aux_upT = (packed[f] for f in ("lo_downT", "aux_down", "lo_upT", "aux_upT"))
        bv_rep = sb("bv_rep", [128, 2, 128])
        lo1 = sb("lo1", [4, 128])
        lo2 = sb("lo2", [50, 128])
        half_neg = sb("half_neg", [128, TT])

        xa = sb("xa", [128, 2, 2, TT, C])
        xr = sb("xr", [128, 2, 2, TT, C])
        x2 = sb("x2", [128, 2, 2, TT, C])
        xn = sb("xn", [128, TT, C])
        xnT = sb("xnT", [128, 4, T])
        qk_raw = sb("qk_raw", [128, 2, T])
        qk_swap = sb("qk_swap", [128, 2, T])
        qk_cos = sb("qk_cos", [128, 2, T])
        qk = sb("qk", [128, 2, 2, T])
        rest = sb("rest", [128, 2, T])
        part = sb("part", [128, 3, 2, T], BF16)
        qs = sb("qs", [KALL + 22, 4, H, T], BF16)
        ks = sb("ks", [KALL + 22, 4, H, T], BF16)
        mx = sb("mx", [128, 2, TT, H])
        mrow = sb("mrow", [H, 2, 2, T], BF16)
        vpad = sb("vpad", [128, 2, TT, 2, 8, 32])
        pt = sb("pt", [128, 4, 4, TT, T])
        o_sb = sb("o_sb", [128, 2, 2, T])
        rs = sb("rs", [128, 32])
        rinv = sb("rinv", [128, 32])
        rb = sb("rb", [128, 2, T])
        ctxn = sb("ctxn", [128, 2, T])
        xb = sb("xb", [128, TT, C])
        x1 = sb("x1", [128, TT, C])
        x1b = sb("x1b", [128, TT, C])
        x1n = sb("x1n", [128, TT, C])
        x1nT = sb("x1nT", [128, T])
        st1 = sb("st1", [128, TT, 6])
        mv1 = sb("mv1", [128, TT, 2])
        ve1 = sb("ve1", [128, TT])
        rstd1 = sb("rstd1", [128, TT])
        st2 = sb("st2", [128, TT, 6])
        mv2 = sb("mv2", [128, TT, 2])
        ve2 = sb("ve2", [128, TT])
        rstd2 = sb("rstd2", [128, TT])

        ps_st = ctx.enter_context(nc.psum_tensor("ps_st", [128, 3, TT, T], F32))
        ps_mx = ctx.enter_context(nc.psum_tensor("ps_mx", [128, 2, TT, T], F32))
        ps_pv = ctx.enter_context(nc.psum_tensor("ps_pv", [128, 2, T], F32))
        ps_small = ctx.enter_context(nc.psum_tensor("ps_small", [128, 2, 512], F32))

        consts_in, fill_in = sem("consts_in"), sem("fill_in")
        setup_pe, setup_dve, setup_pool = sem("setup_pe"), sem("setup_dve"), sem("setup_pool")
        xa_in = sem("xa_in")
        xr_in = sem("xr_in")
        x2_out = sem("x2_out")
        parts_out = sem("parts_out")
        stacks_in = sem("stacks_in")
        mrows_in = sem("mrows_in")
        rsum_in = sem("rsum_in")
        rinv_out = sem("rinv_out")
        rb_in = sem("rb_in")
        aggr1, aggr2 = sem("aggr1"), sem("aggr2")
        stats1, ve1_ok, rstd1_ok, xn_ok = sem("stats1"), sem("ve1_ok"), sem("rstd1_ok"), sem("xn_ok")
        xnT_ps, xnT_ok = sem("xnT_ps"), sem("xnT_ok")
        qk_ps, qk_ok, rope_a, rope_ok = sem("qk_ps"), sem("qk_ok"), sem("rope_a"), sem("rope_ok")
        rest_ok, parts_ok = sem("rest_ok"), sem("parts_ok")
        v_ps, v_ok = sem("v_ps"), sem("v_ok")
        mx_ps = sem("mx_ps")
        mx_ok = sem("mx_ok")
        mrow_ps, mrow1_ok, mrow2_ok = sem("mrow_ps"), sem("mrow1_ok"), sem("mrow2_ok")
        st_ps = sem("st_ps")
        exp_ok = sem("exp_ok")
        pv_ps = sem("pv_ps")
        o_ok, rinv_ok, norm_ok = sem("o_ok"), sem("rinv_ok"), sem("norm_ok")
        y_ps, xb_ok, x1_ok, x1b_ok = sem("y_ps"), sem("xb_ok"), sem("x1_ok"), sem("x1b_ok")
        stats2, ve2_ok, rstd2_ok, x1n_ok = sem("stats2"), sem("ve2_ok"), sem("rstd2_ok"), sem("x1n_ok")
        x1nT_ps, x1nT_ok = sem("x1nT_ps"), sem("x1nT_ok")
        z_ps, x2_ok = sem("z_ps"), sem("x2_ok")

        SMALL = {"xnT": (4, xnT_ok), "mrow": (1, mrow2_ok), "qk": (4, qk_ok), "x1nT": (-3, x1nT_ok),
                 "y": (-2, x1_ok), "v": (1, v_ok), "z": (-3, x2_ok)}
        ORDER = list(SMALL)

        def small(n, name, later=0):
            return ps_small[:, (n.c - later + ORDER.index(name)) % 2]

        def small_bank_free(eng, n, name):
            for at in range(ORDER.index(name) - 2, -3 * len(ORDER), -2):
                off, reader = SMALL[ORDER[at % len(ORDER)]]
                off += at // len(ORDER)
                if n.has(off):
                    return reach(eng, reader, n, 1, off + 1)

        block = ctx.enter_context(nc.Block())

        N_CONST = 16 * len(PACKS)
        N_FIXED = 10

        def pair_of(tensor, n, off):
            view = tensor.rearrange("(g two) (i p) c -> p g two i c", two=2, p=128)
            base = (n.c + off) // 2 % (HALF // 2)
            if n.i is None:
                return view[:, base]
            return view[:, bass.ds(n.i * (UNROLL // 2) + base, 1)].rearrange("p g two i c -> p (g two) i c")

        @block.sync
        def _(sp):
            sp.dma_start(xa[:, 0], pair_of(io["x"], Step(FIRST), -FIRST)).then_inc(xa_in, 16)
            sp.dma_start(packed["pack_first"], io["pack_first"]).then_inc(consts_in, 16)
            sp.dma_start(packed["pack_rows"], io["pack_rows"].partition_broadcast(128)).then_inc(consts_in, 16)
            rows = KALL - 48
            for stack, value in ((qs, 0), (ks, 1)):
                sp.dma_start(stack[48:KALL], io["fill"][value].partition_broadcast(rows)
                             .unsqueeze(1).broadcast_to((rows, 4, H * T))).then_inc(fill_in, 16)
            sp.dma_start(packed["pack_second"], io["pack_second"]).then_inc(consts_in, 16)

            def load_x(n, off, to, done):
                sp.dma_start(to[:, (n.c + off) // 2 % 2], pair_of(mid if n.second(off) else io["x"], n, off)
                             ).then_inc(done, 16)

            def step(n):
                load_xa, load_xr = n.c % 2 == 0 and n.has(6), n.c % 2 and n.has(-1)
                store = n.c % 2 and n.has(-4)
                waits = []
                if n.has(3):
                    reach_all(sp, n, (parts_ok, 1, 4, 0), (stacks_in, 96, 3, 0))
                    sp.dma_start(parts_dram[n.ring(3, 2)].rearrange("s w p t -> p (s w) t"),
                                 part[:, :, :, :].rearrange("p s w t -> p (s w) t")).then_inc(parts_out, 16)
                if n.has(1):
                    waits += [(mrows_in, 32, 1, 0), (mrow1_ok, 1, 2, 0), (mrow2_ok, 1, 2, 0)]
                if load_xa:
                    waits += [(xa_in, 8, 6, 0), (xn_ok, 1, 4, 0)]
                    if n.second(6):
                        waits += [(x2_out, 8, 8 - HALF, 0)]
                if load_xr:
                    waits += [(xr_in, 8, -1, 0), (xb_ok, 1, -3, 0)]
                reach_all(sp, n, *waits)
                if n.has(1):
                    for i in range(2):
                        sp.dma_start(qs[KMAX + i:KMAX + i + 1, n.ring(1, 4)], mrow[:, n.ring(1, 2), i]
                                     ).then_inc(mrows_in, 16)
                if load_xa:
                    load_x(n, 6, xa, xa_in)
                if load_xr:
                    load_x(n, -1, xr, xr_in)
                waits = []
                if n.has(-1):
                    waits += [(rsum_in, 32, -1, 0), (o_ok, 1, 0, 0), (rinv_ok, 1, -1, 0)]
                if store:
                    waits += [(x2_out, 8, -5, 0), (x2_ok, 1, -3, 0)]
                reach_all(sp, n, *waits)
                if n.has(-1):
                    for i in range(2):
                        sp.dma_start(rs[64 * i:64 * i + 64, :], o_sb[16 + i:128:32, n.ring(-1, 2)]
                                     ).then_inc(rsum_in, 16)
                if store:
                    sp.dma_start(pair_of(out if n.second(-4) else mid, n, -5), x2[:, (n.c - 5) // 2 % 2]
                                 ).then_inc(x2_out, 16)
                if n.has(3):
                    reach_all(sp, n,
                              (parts_out, 16, 4, 0),
                              (st_ps, 16, 0, 0))
                    src = parts_dram[n.ring(3, 2)].rearrange("s w (d h) t -> s w d (h t)", d=D)
                    row = 0
                    for a, many in TERM_RUNS:
                        q_src = src[a:a + 1, 0].broadcast_to((many, D, H * T))
                        sp.dma_start(qs[row:row + many * D, n.ring(3, 4)], q_src).then_inc(stacks_in, 16)
                        sp.dma_start(ks[row:row + many * D, n.ring(3, 4)], src[0:many, 1]).then_inc(stacks_in, 16)
                        row += many * D
                if n.has(-1):
                    reach_all(sp, n, (rinv_ok, 1, 0, 0), (rb_in, 32, -1, 0))
                    sp.dma_start(rsum_dram, rinv[:, :]).then_inc(rinv_out, 16)
                    reach_all(sp, n, (rinv_out, 16, 0, 0), (norm_ok, 1, -1, 0))
                    back = rsum_dram.rearrange("(i j c) n -> i j (c n)", i=2, j=4)
                    for i in range(2):
                        sp.dma_start(rb[i:128:2], back[i].unsqueeze(1).broadcast_to((4, 16, 512))
                                     ).then_inc(rb_in, 16)
            steps(sp, step)
            sp.wait_ge(x2_out, 8 * TURNS)

        @block.gpsimd
        def _(pool):
            fixed = [(half_neg[:, :], -0.5), (vpad[:, :, :, :, :, :], 0.0)]
            fixed += [(vpad[:, ring, s, i, :, 16 + i:32:2], 1.0)
                      for i in range(2) for ring in range(2) for s in range(TT)]
            assert len(fixed) == N_FIXED
            for done, (place, value) in enumerate(fixed):
                nc.gpsimd.memset(place, value).then_inc(setup_pool, 1)
                pool.wait_ge(setup_pool, done + 1)
            pool.wait_ge(setup_dve, 5)

            def step(n):
                if n.has(-3):
                    reach(pool, ve2_ok, n, 1, -2)
                    nc.gpsimd.tensor_tensor(rstd2[:, :], ve2[:, :], half_neg[:, :], ALU.pow).then_inc(rstd2_ok, 1)
                if n.has(3):
                    now = qk[:, n.ring(3, 2)]
                    if n.second(3):
                        reach(pool, qk_ok, n, 1, 4)
                    else:
                        reach(pool, rope_ok, n, 1, 4)
                    nc.gpsimd.tensor_tensor(part[:, 1], now, part[:, 0], ALU.subtract)
                    nc.gpsimd.tensor_tensor(rest[:, :, :], now, part[:, 0], ALU.subtract).then_inc(rest_ok, 1)
                    reach(pool, rest_ok, n, 1, 4)
                    nc.gpsimd.tensor_tensor(part[:, 2], rest[:, :, :], part[:, 1], ALU.subtract).then_inc(parts_ok, 1)
                if n.has(5):
                    reach(pool, ve1_ok, n, 1, 6)
                    nc.gpsimd.tensor_tensor(rstd1[:, :], ve1[:, :], half_neg[:, :], ALU.pow).then_inc(rstd1_ok, 1)
                if n.has(-2):
                    reach(pool, rb_in, n, 32, -1)
                    reach(pool, y_ps, n, 1, -2)
                    nc.gpsimd.tensor_tensor(ctxn[:, :, :], o_sb[:, n.ring(-2, 2)], rb[:, :, :], ALU.mult
                                            ).then_inc(norm_ok, 1)
                    if n.c % 2 == 0:
                        reach(pool, xr_in, n, 8, 0)
                    reach(pool, x1_ok, n, 1, -2)
                    bias = bo_rows[int(n.second(-2))].unsqueeze(1).broadcast_to((128, TT, C))
                    nc.gpsimd.tensor_tensor(xb[:, :, :], xr[:, (n.c - 2) // 2 % 2, n.c % 2], bias, ALU.add
                                            ).then_inc(xb_ok, 1)
                if n.has(-3):
                    reach(pool, x2_ok, n, 1, -3)
                    nc.gpsimd.tensor_tensor(x1b[:, :, :], x1[:, :, :],
                                            bf_rows.unsqueeze(1).broadcast_to((128, TT, C)), ALU.add
                                            ).then_inc(x1b_ok, 1)
                if n.has(4) and not n.second(4):
                    reach(pool, qk_ok, n, 1, 5)
                    nc.gpsimd.tensor_tensor(qk_cos[:, :, :], qk_raw[:, :, :], cos_t, ALU.mult)
                    nc.gpsimd.tensor_tensor(qk_swap[:, :, :], qk_swap[:, :, :], sin_t, ALU.mult).then_inc(rope_a, 1)
                    reach(pool, rope_a, n, 1, 5)
                    nc.gpsimd.tensor_tensor(qk[:, n.ring(4, 2)], qk_cos[:, :, :], qk_swap[:, :, :], ALU.add)
                    reach(pool, parts_out, n, 16, 4)
                    nc.gpsimd.tensor_tensor(part[:, 0], qk_cos[:, :, :], qk_swap[:, :, :], ALU.add
                                            ).then_inc(rope_ok, 1)
            steps(pool, step)

        @block.scalar
        def _(act):
            act.wait_ge(consts_in, N_CONST)
            act.wait_ge(setup_pool, N_FIXED)
            act.wait_ge(setup_dve, 5)

            def qk_out(n, w, lot):
                src = small(n, "qk")[:, w * T:(w + 1) * T]
                if n.second(4):
                    to = part[:, 0, w] if lot == 1 else qk[:, n.ring(4, 2), w]
                    return nc.scalar.activation(to, src, ACT.Identity, scale=scal[:, w:w + 1],
                                                bias=cols[1][:, w:w + 1])
                if lot == 0:
                    return nc.scalar.activation(qk_raw[:, w], src, ACT.Identity, bias=cols[0][:, w:w + 1])
                to, of = (slice(0, 64), slice(64, 128)) if lot == 1 else (slice(64, 128), slice(0, 64))
                return nc.scalar.activation(qk_swap[to, w], src[of], ACT.Identity, bias=cols[0][of, w:w + 1])

            def step(n):
                for h in range(H):
                    if n.has(0):
                        u = h // 4
                        act.wait_ge(st_ps, n.lin(16, 0, h + 1))
                        if h % 4 == 0:
                            reach(act, pv_ps, n, 4, -1, u + 1)
                        nc.scalar.activation(pt[:, u, h % 4], ps_st[:, ST_BANK[h]], ACT.Exp,
                                             scale=float(D) ** -0.5).then_inc(exp_ok, 1)
                    if h == 1 and n.has(4):
                        reach(act, xnT_ps, n, 1, 5)
                        reach(act, v_ps, n, 1, 1)
                        nc.scalar.activation(xnT[:, n.ring(4, 4)], small(n, "xnT")[:, 0:T], ACT.Copy
                                             ).then_inc(xnT_ok, 1)
                    if h == 3 and n.has(1):
                        reach(act, mrow_ps, n, 1, 2)
                        reach(act, mrows_in, n, 32, 0)
                        nc.scalar.activation(mrow[:, n.ring(1, 2), 0], small(n, "mrow")[0:H, 0:T], ACT.Copy
                                             ).then_inc(mrow1_ok, 1)
                    if h == 4 and n.has(-1):
                        reach(act, pv_ps, n, 4, 0)
                        reach(act, norm_ok, n, 1, -2)
                        nc.scalar.activation(o_sb[:, n.ring(-1, 2)], ps_pv[:, :, :], ACT.Copy).then_inc(o_ok, 1)
                    if n.has(4) and h in (5, 6, 8)[:2 if n.second(4) else 3]:
                        if h == 5:
                            reach(act, qk_ps, n, 1, 5)
                            if n.second(4):
                                reach(act, parts_ok, n, 1, 3)
                            else:
                                reach(act, rope_ok, n, 1, 4)
                        if n.second(4) and h == 6:
                            reach(act, parts_out, n, 16, 4)
                        lot = (5, 6, 8).index(h)
                        qk_out(n, 0, lot)
                        last = qk_out(n, 1, lot)
                        if lot == (1 if n.second(4) else 2):
                            last.then_inc(qk_ok, 1)
                    if h == 9 and n.has(-3):
                        reach(act, x1nT_ps, n, 1, -2)
                        reach(act, z_ps, n, 1, -3)
                        nc.scalar.activation(x1nT[:, :], small(n, "x1nT")[:, 0:T], ACT.Copy).then_inc(x1nT_ok, 1)
                    if h == 13 and n.has(1):
                        reach(act, v_ps, n, 1, 2)
                        reach(act, pv_ps, n, 4, 0)
                        scale = scal[:, 2:3] if n.second(1) else 1.0
                        src = small(n, "v")[:, 0:TT * C].rearrange("p (s i h d) -> p s i h d", s=TT, i=2, h=8)
                        for i in range(2):
                            last = nc.scalar.activation(vpad[:, n.ring(1, 2), :, i, :, i:16:2], src[:, :, i],
                                                        ACT.Identity, scale=scale)
                        last.then_inc(v_ok, 1)
            steps(act, step)

        @block.vector
        def _(dve):
            dve.wait_ge(consts_in, N_CONST)
            dve.wait_ge(setup_pe, 1)
            nc.vector.tensor_copy(lo1[:, :], ps_small[0:4, 0, 0:128]).then_inc(setup_dve, 1)
            for a in range(2):
                nc.vector.tensor_copy(bv_rep[:, a], cols[a][:, 2:3].broadcast_to((128, 128)))
            dve.wait_ge(setup_pe, 2)
            nc.vector.tensor_copy(lo2[:, :], ps_small[0:50, 0, 0:128]).then_inc(setup_dve, 1)
            dve.wait_ge(setup_pe, 3)
            nc.vector.tensor_tensor(wfT, ps_small[:, 0, 0:128], wfT, ALU.add).then_inc(setup_dve, 1)
            dve.wait_ge(setup_pe, 4)
            nc.vector.tensor_tensor(bo_rows[0], ps_small[:, 0, 0:128], bo_rows[0], ALU.add).then_inc(setup_dve, 1)
            nc.vector.scalar_tensor_tensor(bo_rows[1], ps_small[:, 0, 128:256], scal[:, 3:4], bo_rows[1],
                                           ALU.mult, ALU.add).then_inc(setup_dve, 1)

            def statistics(x, stat, done, tile):
                last = nc.vector.bn_stats(stat[:, tile, :], x[:, tile, :])
                if tile == TT - 1:
                    last.then_inc(done, 1)

            def variance(stat, mv, ve, n, off, stats_sem, aggr_sem, ve_sem):
                for i in range(TT):
                    last = nc.vector.bn_aggr(mv[:, i, :], stat[:, i, :])
                last.then_inc(aggr_sem, 1)
                reach(dve, aggr_sem, n, 1, off, 1)
                nc.vector.tensor_scalar(ve[:, :], mv[:, :, 1], LN_EPS, None, ALU.add).then_inc(ve_sem, 1)

            def tiles(bank):
                return bank[:, 0:TT * C].rearrange("p (i c) -> p i c", i=TT)

            def step(n):
                xa_now = xa[:, (n.c + 5) // 2 % 2, (n.c + 5) % 2]
                for h in range(H):
                    if h == 2 and n.has(5):
                        reach(dve, stats1, n, 1, 6)
                    if h == 14 and n.has(-2):
                        reach(dve, stats2, n, 1, -1)
                    if n.has(2):
                        if h == 0:
                            reach(dve, mrow_ps, n, 1, 1)
                        dve.wait_ge(mx_ps, n.lin(16, 2, h + 1))
                        nc.vector.tensor_reduce(mx[:, n.ring(2, 2), :, h], ps_mx[:, h % 2], AX, ALU.max,
                                                negate=True).then_inc(mx_ok, 1)
                    if h == 4 and n.has(1):
                        reach(dve, mrow1_ok, n, 1, 2)
                        nc.vector.tensor_tensor(mrow[:, n.ring(1, 2), 1], small(n, "mrow")[0:H, 0:T],
                                                mrow[:, n.ring(1, 2), 0], ALU.subtract).then_inc(mrow2_ok, 1)
                    if h in (5, 6) and n.has(-3):
                        if h == 5:
                            reach(dve, rstd2_ok, n, 1, -2)
                            reach(dve, x1nT_ps, n, 1, -3)
                        last = nc.vector.tensor_scalar(x1n[:, h - 5], x1[:, h - 5], mv2[:, h - 5, 0:1],
                                                       rstd2[:, h - 5:h - 4], ALU.subtract, ALU.mult)
                        if h == 6:
                            last.then_inc(x1n_ok, 1)
                    if h in (0, 1) and n.has(5):
                        if h == 0 and n.c % 2:
                            reach(dve, xa_in, n, 8, 7)
                        statistics(xa_now, st1, stats1, h)
                    if h == 2 and n.has(5):
                        variance(st1, mv1, ve1, n, 5, stats1, aggr1, ve1_ok)
                    if h in (8, 9) and n.has(5):
                        if h == 8:
                            reach(dve, rstd1_ok, n, 1, 6)
                            reach(dve, xnT_ps, n, 1, 5)
                        last = nc.vector.tensor_scalar(xn[:, h - 8], xa_now[:, h - 8], mv1[:, h - 8, 0:1],
                                                       rstd1[:, h - 8:h - 7], ALU.subtract, ALU.mult)
                        if h == 9:
                            last.then_inc(xn_ok, 1)
                    if h == 10 and n.has(-1):
                        reach(dve, rsum_in, n, 32, 0)
                        reach(dve, rinv_out, n, 16, -1)
                        nc.vector.reciprocal(rinv[:, :], rs[:, :]).then_inc(rinv_ok, 1)
                    if h == 11 and n.has(-2):
                        reach(dve, y_ps, n, 1, -1)
                        reach(dve, xb_ok, n, 1, -1)
                        reach(dve, x1b_ok, n, 1, -2)
                        y = tiles(small(n, "y"))
                        if n.second(-2):
                            nc.vector.scalar_tensor_tensor(x1[:, :, :], y, scal[:, 3:4], xb[:, :, :],
                                                           ALU.mult, ALU.add).then_inc(x1_ok, 1)
                        else:
                            nc.vector.tensor_tensor(x1[:, :, :], y, xb[:, :, :], ALU.add).then_inc(x1_ok, 1)
                    if h in (12, 13) and n.has(-2):
                        if h == 12:
                            reach(dve, x1_ok, n, 1, -1)
                        statistics(x1, st2, stats2, h - 12)
                    if h == 14 and n.has(-2):
                        variance(st2, mv2, ve2, n, -2, stats2, aggr2, ve2_ok)
                    if h == 15 and n.has(-3):
                        reach(dve, x1b_ok, n, 1, -2)
                        reach(dve, z_ps, n, 1, -2)
                        if n.c % 2:
                            reach(dve, x2_out, n, 8, -5)
                        nc.vector.tensor_tensor(x2[:, (n.c - 3) // 2 % 2, (n.c - 3) % 2], tiles(small(n, "z")),
                                                x1b[:, :, :], ALU.add).then_inc(x2_ok, 1)
            steps(dve, step)

        @block.tensor
        def _(pe):
            mm = nc.tensor.matmul
            pe.wait_ge(consts_in, N_CONST)
            mm(ps_small[0:4, 0, 0:128], lo_downT, aux_down, start=True, stop=True).then_inc(setup_pe, 1)
            pe.wait_ge(setup_dve, 1)
            mm(ps_small[0:50, 0, 0:128], lo_upT, lo1[:, :], start=True, stop=True).then_inc(setup_pe, 1)
            pe.wait_ge(setup_dve, 2)
            mm(ps_small[:, 0, 0:128], lo2[:, :], aux_upT, start=True, stop=True).then_inc(setup_pe, 1)
            pe.wait_ge(setup_dve, 3)
            for a in range(2):
                last = mm(ps_small[:, 0, a * 128:a * 128 + 128], bv_rep[:, a], woT[a], start=True, stop=True)
            last.then_inc(setup_pe, 1)
            pe.wait_ge(setup_dve, 5)
            pe.wait_ge(fill_in, 32)
            pe.wait_ge(setup_pool, N_FIXED)

            def key_major_scores(n, h):
                if h == 0:
                    reach(pe, mrows_in, n, 32, 1)
                reach(pe, exp_ok, n, 16, 0, ST_BEFORE[h] + 1)
                r = n.ring(0, 4)
                for s in range(TT):
                    last = mm(ps_st[:, ST_BANK[h], s], ks[0:KALL, r, h, s * 128:s * 128 + 128],
                              qs[0:KALL, r, h, :], start=True, stop=True)
                last.then_inc(st_ps, 1)

            def token_major_scores(n, h):
                if h == 0:
                    reach(pe, stacks_in, n, 96, 3)
                r = n.ring(2, 4)
                reach(pe, mx_ok, n, 16, 2, h - 1)
                for i in range(TT):
                    last = mm(ps_mx[:, h % 2, i], qs[0:KMAX, r, h, i * 128:i * 128 + 128],
                              ks[0:KMAX, r, h, :], start=True, stop=True)
                last.then_inc(mx_ps, 1)

            def times_v(n, off, u, s):
                i, r = u % 2, u // 2
                if s == 0:
                    reach(pe, exp_ok, n, 16, off, 4 * u + 4)
                    if u == 0:
                        reach(pe, v_ok, n, 1, off + 1)
                        reach(pe, o_ok, n, 1, off)
                for j in range(4):
                    last = mm(ps_pv[32 * j:32 * j + 32, r], vpad[:, n.ring(off, 2), s, i, r * 4 + j, :],
                              pt[:, u, j, s], start=(i == 0 and s == 0), stop=(i == 1 and s == 1))
                if s == 1:
                    last.then_inc(pv_ps, 1)

            def small_product(n, name):
                off, _ = SMALL[name]
                if not n.has(off):
                    return
                bank, a = small(n, name), int(n.second(off))
                small_bank_free(pe, n, name)
                if name == "xnT":
                    reach(pe, xn_ok, n, 1, 5)
                    for i in range(TT):
                        last = nc.tensor.transpose(bank[:, i * 128:i * 128 + 128], xn[:, i], ident)
                    last.then_inc(xnT_ps, 1)
                if name == "mrow":
                    reach(pe, mx_ok, n, 16, 2)
                    for i in range(TT):
                        last = nc.tensor.transpose(bank[0:H, i * 128:i * 128 + 128], mx[:, n.ring(1, 2), i, :], ident)
                    last.then_inc(mrow_ps, 1)
                if name == "qk":
                    reach(pe, xnT_ok, n, 1, 5)
                    for w, weight in enumerate((wqT, wkT)):
                        last = mm(bank[:, w * T:(w + 1) * T], weight[a], xnT[:, n.ring(4, 4)], start=True, stop=True)
                    last.then_inc(qk_ps, 1)
                if name == "x1nT":
                    reach(pe, x1n_ok, n, 1, -2)
                    for i in range(TT):
                        last = nc.tensor.transpose(bank[:, i * 128:i * 128 + 128], x1n[:, i], ident)
                    last.then_inc(x1nT_ps, 1)
                if name == "y":
                    reach(pe, norm_ok, n, 1, -1)
                    for i in range(TT):
                        for r in range(2):
                            last = mm(bank[:, i * C:i * C + C], ctxn[:, r, i * 128:i * 128 + 128], woP[a][r],
                                      start=(r == 0), stop=(r == 1))
                    last.then_inc(y_ps, 1)
                if name == "v":
                    for i in range(TT):
                        last = mm(bank[:, i * C:i * C + C], xnT[:, n.ring(1, 4), i * 128:i * 128 + 128], wvT[a],
                                  start=True, stop=True)
                    last.then_inc(v_ps, 1)
                if name == "z":
                    reach(pe, x1nT_ok, n, 1, -2)
                    for i in range(TT):
                        last = mm(bank[:, i * C:i * C + C], x1nT[:, i * 128:i * 128 + 128], wfT,
                                  start=True, stop=True)
                    last.then_inc(z_ps, 1)

            QUADS_AT = [[(-1, 2, 1), (-1, 3, 0)], [(-1, 3, 1)], [], [(0, 0, 0)], [(0, 0, 1)], [(0, 1, 0)],
                        [(0, 1, 1)], [(0, 2, 0)]]
            AT_SLOT = {0: "xnT", 1: "mrow", 2: "qk", 4: "x1nT", 5: "y", 6: "v", 7: "z"}

            def step(n):
                for k in range(SLOTS):
                    for h in (2 * k, 2 * k + 1):
                        if n.has(0):
                            key_major_scores(n, h)
                        if h % 2 == 0 and k in AT_SLOT:
                            small_product(n, AT_SLOT[k])
                        if n.has(2):
                            token_major_scores(n, h)
                    for off, u, s in QUADS_AT[k]:
                        if n.has(off):
                            times_v(n, off, u, s)
            steps(pe, step)


def kernel(**inputs):
    import numpy as np
    import concourse.bacc as bacc
    from concourse.bass_utils import run_bass_kernel_spmd

    g = {k: np.asarray(v) for k, v in inputs.items()}
    a, b, f = "L0_attn_a_", "L0_attn_b_", "L0_ffn_"
    names = [(a + "Wq", a + "Wk", a + "Wv", a + "Wo", a + "bq", a + "bk", a + "bv", a + "bo"),
             (b + "w_q", b + "w_k", b + "w_v", b + "w_o", b + "b_q", b + "b_k", b + "b_v", b + "b_o")]
    qk_order = np.array([8 * h + d for d in range(8) for h in range(16)])
    head = lambda i, r, j: 4 * (2 * r + i) + j
    v_order = np.array([8 * head(i, r, j) + d for i in range(2) for r in range(2) for j in range(4) for d in range(8)])
    inv_freq = (1.0 / 10000.0 ** (np.arange(0, 8, 2, dtype=np.float32) / 8)).astype(np.float32)
    angle = np.arange(256, dtype=np.float32)[None, :] * inv_freq[:, None]
    cos_t = np.repeat(np.cos(angle), 16, axis=0)
    sin_t = np.repeat(np.sin(angle), 16, axis=0)
    cos_t = np.concatenate([cos_t, cos_t]).astype(np.float32)
    sin_t = np.concatenate([-sin_t, sin_t]).astype(np.float32)
    fields = {
        "ident": np.eye(128, dtype=np.float32),
        "cos_t": np.concatenate([cos_t, cos_t], axis=1), "sin_t": np.concatenate([sin_t, sin_t], axis=1),
        "wfT": g[f + "W"].T, "lo_downT": g[f + "lora_down"].T, "aux_down": g[f + "down_aux"],
        "lo_upT": g[f + "lora_up"].T, "aux_upT": g[f + "up_aux"].T, "bf": g[f + "b"],
        "scal": np.stack([g[b + "s_q"], g[b + "s_k"], g[b + "s_v"], g[b + "s_o"]]).reshape(4),
    }
    for n, (wq, wk, wv, wo, bq, bk, bv, bo) in enumerate(names):
        fields[f"wqT{n}"] = g[wq][qk_order].T
        fields[f"wkT{n}"] = g[wk][qk_order].T
        fields[f"wvT{n}"] = g[wv][v_order].T
        fields[f"woT{n}"] = g[wo].T
        fields[f"cols{n}"] = np.stack([g[bq][qk_order], g[bk][qk_order], g[bv]], axis=1)
        fields[f"bo{n}"] = g[bo]
        for r in range(2):
            padded = np.zeros((128, 128), np.float32)
            for i in range(2):
                for j in range(4):
                    padded[32 * j + i:32 * j + 16:2] = g[wo].T[8 * head(i, r, j):8 * head(i, r, j) + 8]
            fields[f"woP{n}{r}"] = padded
    arrays = {"x": g[a + "x"],
              "fill": np.stack([np.zeros(H * T), np.ones(H * T)]).astype(mybir.dt.np(mybir.dt.bfloat16))}
    for name, pack in PACKS.items():
        if name == "pack_rows":
            arrays[name] = np.concatenate([fields[field] for field, _, _ in pack])
            continue
        tile = np.zeros((128, sum(width for _, _, width in pack)), np.float32)
        at = 0
        for field, rows, width in pack:
            tile[0:rows, at:at + width] = fields[field]
            at += width
        arrays[name] = tile
    arrays = {f"in_{k}": np.ascontiguousarray(v) for k, v in arrays.items()}

    nc = bacc.Bacc("TRN2", target_bir_lowering=False, num_devices=1)
    io = {k[3:]: nc.dram_tensor(k, v.shape, mybir.dt.from_np(v.dtype), kind="ExternalInput").ap()
          for k, v in arrays.items()}
    out = nc.dram_tensor("out", (32, 256, 128), mybir.dt.float32, kind="ExternalOutput").ap()
    build(nc, io, out)
    r = run_bass_kernel_spmd(nc, [arrays], core_ids=[0])
    return r.results[0]["out"]
```

```python
import concourse.bass as bass
from concourse import mybir
from contextlib import ExitStack

TURNS, HALF = 64, 32
T, C, H, D = 256, 128, 16, 8
TT = T // 128
PARTS = 3
KMAX = PARTS * PARTS * D
KALL = KMAX + 2
LN_EPS = 1e-5
FIRST, LAST = -5, TURNS + 3
SETUP_STEP = FIRST + 2
UNROLL = 4
SEGMENTS = [(FIRST, 11, False), (6, 20, True), (26, 11, False), (37, 20, True), (57, 11, False)]
assert SEGMENTS[-1][0] + SEGMENTS[-1][1] - 1 == LAST

PE_AT = {"z": 0, "xnT": 1, "mrow": 3, "q": 5, "k": 5, "x1nT": 9, "y0": 12, "y1": 12, "v": 13}
ACT_AT = {"xnT": 3, "o_sb": 3, "mrow": 3, "x1nT": 9, "v": 13}
DVE_AT = {"var2": 2, "mxp1": 0, "mxp2": 1, "x2": 1, "st1_0": 2, "st1_1": 3, "var1": 4, "x1n_0": 5, "x1n_1": 6,
          "xn_0": 7, "xn_1": 8, "recip": 10, "x1": 12, "st2_0": 14, "st2_1": 15}
QK_OUT_AT = [{(0, 0): 5, (1, 0): 6, (0, 1): 7, (1, 1): 7, (0, 2): 9, (1, 2): 9},
             {(0, 0): 6, (1, 0): 7, (0, 1): 8, (1, 1): 9}]
QUADS_AT = {(0, 0): 6, (0, 1): 7, (1, 0): 9, (1, 1): 10, (2, 0): 14, (2, 1): 17, (3, 0): 18, (3, 1): 19}
POOL_ORDER = ["splits", "rstd2", "rstd1", "norm", "x1b", "xb", "rope"]
SP_ORDER = ["parts", "rows", "sums", "stacks", "reciprocals"]

ST_BANK = [0, 1, 2] * 5 + [1]
ST_BEFORE = [max(j for j in range(-H, h) if ST_BANK[j % H] == ST_BANK[h]) for h in range(H)]


class Step:

    def __init__(self, c, i=None):
        self.c, self.i = c, i

    def has(self, off):
        return 0 <= self.c + off < TURNS

    def second(self, off):
        return self.c + off >= HALF

    def ring(self, off, size):
        return (self.c + off) % size

    def lin(self, per, off, extra=0):
        base = per * (self.c + off) + extra
        return base if self.i is None else self.i * (UNROLL * per) + base


def reach(eng, sem, n, per, off, extra=0):
    if per * (n.c + off) + extra > 0:
        eng.wait_ge(sem, n.lin(per, off, extra))


def reach_all(eng, n, *targets):
    values = [(sem, n.lin(per, off, extra)) for sem, per, off, extra in targets if per * (n.c + off) + extra > 0]
    if n.i is not None:
        values = [(sem, eng.to_reg(value)) for sem, value in values]
    for sem, value in values:
        eng.wait_ge(sem, value)


def steps(eng, body):
    for first, count, looped in SEGMENTS:
        if looped:
            with eng.Fori(0, count // UNROLL) as i:
                for u in range(UNROLL):
                    body(Step(first + u, i))
        else:
            for c in range(first, first + count):
                body(Step(c))


PACKS = {
    "pack_first": [("ident", 128, 128), ("wqT0", 128, 128), ("wkT0", 128, 128), ("cols0", 128, 3), ("cols1", 128, 3),
                   ("lo_downT", 100, 4), ("aux_down", 100, 128), ("lo_upT", 4, 50), ("aux_upT", 50, 128),
                   ("wfT", 128, 128)],
    "pack_second": [("cos_t", 128, 512), ("sin_t", 128, 512), ("wqT1", 128, 128), ("wkT1", 128, 128)]
                   + [(f"{w}{a}{r}", 128, 128) for a in range(2)
                      for w, r in (("wvT", ""), ("woT", ""), ("woP", 0), ("woP", 1))],
    "pack_rows": [("bo0", 128, 128), ("bo1", 128, 128), ("bf", 128, 128), ("scal", 128, 4)],
}


def build(nc, io, out):
    F32, BF16 = mybir.dt.float32, mybir.dt.bfloat16
    ALU, ACT, AX = mybir.AluOpType, mybir.ActivationFunctionType, mybir.AxisListType.X

    ctx = ExitStack()
    with ctx:
        def sb(name, shape, dt=F32):
            return ctx.enter_context(nc.sbuf_tensor(name, shape, dt))

        def sem(name):
            return ctx.enter_context(nc.semaphore(name))

        mid = nc.dram_tensor("mid", [HALF, T, C], F32, kind="Internal").ap()
        parts_dram = nc.dram_tensor("parts_dram", [2, 3, 2, 128, T], BF16, kind="Internal").ap()
        rsum_dram = nc.dram_tensor("rsum_dram", [128, 32], F32, kind="Internal").ap()

        packed = {}
        for name, fields in PACKS.items():
            tile = sb(name, [128, sum(width for _, _, width in fields)])
            at = 0
            for field, rows, width in fields:
                packed[field] = tile[0:rows, at:at + width]
                at += width
            packed[name] = tile[:, :]
        ident, wfT = packed["ident"], packed["wfT"]
        cos_t, sin_t = (packed[f].rearrange("p (w t) -> p w t", w=2) for f in ("cos_t", "sin_t"))
        wqT, wkT, wvT, woT, cols, bo_rows = ([packed[f"{f}{a}"] for a in range(2)]
                                             for f in ("wqT", "wkT", "wvT", "woT", "cols", "bo"))
        woP = [[packed[f"woP{a}{r}"] for r in range(2)] for a in range(2)]
        bf_rows, scal = packed["bf"], packed["scal"]
        lo_downT, aux_down, lo_upT, aux_upT = (packed[f] for f in ("lo_downT", "aux_down", "lo_upT", "aux_upT"))
        bv_rep = sb("bv_rep", [128, 2, 128])
        lo1 = sb("lo1", [4, 128])
        lo2 = sb("lo2", [50, 128])
        half_neg = sb("half_neg", [128, TT])

        xa = sb("xa", [128, 2, 2, TT, C])
        xr = sb("xr", [128, 2, 2, TT, C])
        x2 = sb("x2", [128, 2, 2, TT, C])
        xn = sb("xn", [128, TT, C])
        xnT = sb("xnT", [128, 4, T])
        qk_raw = sb("qk_raw", [128, 2, T])
        qk_swap = sb("qk_swap", [128, 2, T])
        qk_cos = sb("qk_cos", [128, 2, T])
        qk = sb("qk", [128, 2, 2, T])
        rest = sb("rest", [128, 2, T])
        part = sb("part", [128, 3, 2, T], BF16)
        qs = sb("qs", [KALL, 4, H, T], BF16)
        ks = sb("ks", [KALL, 4, H, T], BF16)
        mx = sb("mx", [128, 2, TT, H])
        mxp = sb("mxp", [128, TT, 2, H], BF16)
        mrow = sb("mrow", [2 * H, 2, T], BF16)
        ident_bf = sb("ident_bf", [128, 128], BF16)
        vpad = sb("vpad", [128, 2, TT, 2, 8, 32])
        pt = sb("pt", [128, 4, 4, TT, T])
        o_sb = sb("o_sb", [128, 2, 2, T])
        rs = sb("rs", [128, 32])
        rinv = sb("rinv", [128, 32])
        rb = sb("rb", [128, 2, T])
        ctxn = sb("ctxn", [128, 2, T])
        xb = sb("xb", [128, TT, C])
        x1 = sb("x1", [128, TT, C])
        x1b = sb("x1b", [128, TT, C])
        x1n = sb("x1n", [128, TT, C])
        x1nT = sb("x1nT", [128, T])
        st1 = sb("st1", [128, TT, 6])
        mv1 = sb("mv1", [128, TT, 2])
        ve1 = sb("ve1", [128, TT])
        rstd1 = sb("rstd1", [128, TT])
        st2 = sb("st2", [128, TT, 6])
        mv2 = sb("mv2", [128, TT, 2])
        ve2 = sb("ve2", [128, TT])
        rstd2 = sb("rstd2", [128, TT])

        ps_st = ctx.enter_context(nc.psum_tensor("ps_st", [128, 3, TT, T], F32))
        ps_mx = ctx.enter_context(nc.psum_tensor("ps_mx", [128, 2, TT, T], F32))
        ps_pv = ctx.enter_context(nc.psum_tensor("ps_pv", [128, 2, T], F32))
        ps_small = ctx.enter_context(nc.psum_tensor("ps_small", [128, 2, 512], F32))

        first_in, consts_in, fill_in = sem("first_in"), sem("consts_in"), sem("fill_in")
        setup_pe, setup_dve, setup_pool = sem("setup_pe"), sem("setup_dve"), sem("setup_pool")
        xa_in = sem("xa_in")
        xr_in = sem("xr_in")
        x2_out = sem("x2_out")
        parts_out = sem("parts_out")
        stacks_in = sem("stacks_in")
        mrows_in = sem("mrows_in")
        rsum_in = sem("rsum_in")
        rinv_out = sem("rinv_out")
        rb_in = sem("rb_in")
        aggr1, aggr2 = sem("aggr1"), sem("aggr2")
        stats1, ve1_ok, rstd1_ok, xn_ok = sem("stats1"), sem("ve1_ok"), sem("rstd1_ok"), sem("xn_ok")
        xnT_ps, xnT_ok = sem("xnT_ps"), sem("xnT_ok")
        qk_ps, qk_ok, rope_a, rope_ok = sem("qk_ps"), sem("qk_ok"), sem("rope_a"), sem("rope_ok")
        rest_ok, parts_ok = sem("rest_ok"), sem("parts_ok")
        v_ps, v_ok = sem("v_ps"), sem("v_ok")
        mx_ps = sem("mx_ps")
        mx_ok = sem("mx_ok")
        mxp1_ok, mxp_ok, mrow_ps, mrow_ok = sem("mxp1_ok"), sem("mxp_ok"), sem("mrow_ps"), sem("mrow_ok")
        st_ps = sem("st_ps")
        exp_ok = sem("exp_ok")
        pv_ps = sem("pv_ps")
        o_ok, rinv_ok, norm_ok = sem("o_ok"), sem("rinv_ok"), sem("norm_ok")
        y_ps, xb_ok, x1_ok, x1b_ok = sem("y_ps"), sem("xb_ok"), sem("x1_ok"), sem("x1b_ok")
        stats2, ve2_ok, rstd2_ok, x1n_ok = sem("stats2"), sem("ve2_ok"), sem("rstd2_ok"), sem("x1n_ok")
        x1nT_ps, x1nT_ok = sem("x1nT_ps"), sem("x1nT_ok")
        z_ps, x2_ok = sem("z_ps"), sem("x2_ok")

        SMALL = {"z": (-4, x2_ok), "xnT": (4, xnT_ok), "mrow": (1, mrow_ok), "qk": (4, qk_ok),
                 "x1nT": (-3, x1nT_ok), "y": (-2, x1_ok), "v": (1, v_ok)}
        ORDER = sorted(SMALL, key=lambda name: PE_AT[{"qk": "q", "y": "y0"}.get(name, name)])

        def small(n, name):
            return ps_small[:, (n.c + ORDER.index(name)) % 2]

        def small_bank_free(eng, n, name):
            for at in range(ORDER.index(name) - 2, -3 * len(ORDER), -2):
                off, reader = SMALL[ORDER[at % len(ORDER)]]
                off += at // len(ORDER)
                if n.has(off):
                    return reach(eng, reader, n, 1, off + 1)

        block = ctx.enter_context(nc.Block())

        N_CONST = 16 * (len(PACKS) - 1)
        N_FIXED = 10

        def pair_of(tensor, n, off):
            view = tensor.rearrange("(g two) (i p) c -> p g two i c", two=2, p=128)
            base = (n.c + off) // 2 % (HALF // 2)
            if n.i is None:
                return view[:, base]
            return view[:, bass.ds(n.i * (UNROLL // 2) + base, 1)].rearrange("p g two i c -> p (g two) i c")

        @block.sync
        def _(sp):
            sp.dma_start(xa[:, 0], pair_of(io["x"], Step(FIRST), -FIRST)).then_inc(xa_in, 16)
            sp.dma_start(packed["pack_first"], io["pack_first"]).then_inc(first_in, 16)
            sp.dma_start(packed["pack_second"], io["pack_second"]).then_inc(consts_in, 16)
            sp.dma_start(packed["pack_rows"], io["pack_rows"].partition_broadcast(128)).then_inc(consts_in, 16)
            sp.dma_start(ks[KMAX:KALL], io["ones"].partition_broadcast(KALL - KMAX)
                         .unsqueeze(1).broadcast_to((KALL - KMAX, 4, H * T))).then_inc(fill_in, 16)

            def load_x(n, off, to, done):
                sp.dma_start(to[:, (n.c + off) // 2 % 2], pair_of(mid if n.second(off) else io["x"], n, off)
                             ).then_inc(done, 16)

            def step(n, job):
                if job == "parts" and n.has(3):
                    reach_all(sp, n, (parts_ok, 1, 4, 0), (stacks_in, 96, 3, 0))
                    sp.dma_start(parts_dram[n.ring(3, 2)].rearrange("s w p t -> p (s w) t"),
                                 part[:, :, :, :].rearrange("p s w t -> p (s w) t")).then_inc(parts_out, 16)
                if job == "rows":
                    load_xa, load_xr = n.c % 2 == 0 and n.has(6), n.c % 2 and n.has(-1)
                    waits = []
                    if n.has(1):
                        waits += [(mrows_in, 16, 1, 0), (mrow_ok, 1, 2, 0)]
                    if load_xa:
                        waits += [(xa_in, 8, 6, 0), (xn_ok, 1, 4, 0)]
                        if n.second(6):
                            waits += [(x2_out, 8, 8 - HALF, 0)]
                    if load_xr:
                        waits += [(xr_in, 8, -1, 0), (xb_ok, 1, -3, 0)]
                    reach_all(sp, n, *waits)
                    if n.has(1):
                        sp.dma_start(qs[KMAX:KALL, n.ring(1, 4)], mrow[:, n.ring(1, 2)]).then_inc(mrows_in, 16)
                    if load_xa:
                        load_x(n, 6, xa, xa_in)
                    if load_xr:
                        load_x(n, -1, xr, xr_in)
                if job == "sums":
                    store = n.c % 2 and n.has(-4)
                    waits = []
                    if n.has(-1):
                        waits += [(rsum_in, 32, -1, 0), (o_ok, 1, 0, 0), (rinv_ok, 1, -1, 0)]
                    if store:
                        waits += [(x2_out, 8, -5, 0), (x2_ok, 1, -3, 0)]
                    reach_all(sp, n, *waits)
                    if n.has(-1):
                        for i in range(2):
                            sp.dma_start(rs[64 * i:64 * i + 64, :], o_sb[16 + i:128:32, n.ring(-1, 2)]
                                         ).then_inc(rsum_in, 16)
                    if store:
                        sp.dma_start(pair_of(out if n.second(-4) else mid, n, -5), x2[:, (n.c - 5) // 2 % 2]
                                     ).then_inc(x2_out, 16)
                if job == "stacks" and n.has(3):
                    reach_all(sp, n,
                              (parts_out, 16, 4, 0),
                              (st_ps, 16, 0, 0))
                    src = parts_dram[n.ring(3, 2)].rearrange("s w (d h) t -> s w d (h t)", d=D)
                    for a in range(PARTS):
                        rows = slice(a * PARTS * D, (a + 1) * PARTS * D)
                        q_src = src[a:a + 1, 0].broadcast_to((PARTS, D, H * T))
                        sp.dma_start(qs[rows, n.ring(3, 4)], q_src).then_inc(stacks_in, 16)
                        sp.dma_start(ks[rows, n.ring(3, 4)], src[:, 1]).then_inc(stacks_in, 16)
                if job == "reciprocals" and n.has(-1):
                    reach_all(sp, n, (rinv_ok, 1, 0, 0), (rb_in, 32, -1, 0))
                    sp.dma_start(rsum_dram, rinv[:, :]).then_inc(rinv_out, 16)
                    reach_all(sp, n, (rinv_out, 16, 0, 0), (norm_ok, 1, -1, 0))
                    back = rsum_dram.rearrange("(i j c) n -> i j (c n)", i=2, j=4)
                    for i in range(2):
                        sp.dma_start(rb[i:128:2], back[i].unsqueeze(1).broadcast_to((4, 16, 512))
                                     ).then_inc(rb_in, 16)
            def all_jobs(n):
                for job in SP_ORDER:
                    step(n, job)
            steps(sp, all_jobs)
            sp.wait_ge(x2_out, 8 * TURNS)

        @block.gpsimd
        def _(pool):
            fixed = [(half_neg[:, :], -0.5), (vpad[:, :, :, :, :, :], 0.0)]
            fixed += [(vpad[:, ring, s, i, :, 16 + i:32:2], 1.0)
                      for i in range(2) for ring in range(2) for s in range(TT)]
            assert len(fixed) == N_FIXED
            for done, (place, value) in enumerate(fixed):
                nc.gpsimd.memset(place, value).then_inc(setup_pool, 1)
                pool.wait_ge(setup_pool, done + 1)

            def step(n, job):
                if job == "rstd2" and n.has(-3):
                    reach(pool, ve2_ok, n, 1, -2)
                    nc.gpsimd.tensor_tensor(rstd2[:, :], ve2[:, :], half_neg[:, :], ALU.pow).then_inc(rstd2_ok, 1)
                if job == "splits" and n.has(3):
                    now = qk[:, n.ring(3, 2)]
                    if n.second(3):
                        reach(pool, qk_ok, n, 1, 4)
                    else:
                        reach(pool, rope_ok, n, 1, 4)
                    nc.gpsimd.tensor_tensor(part[:, 1], now, part[:, 0], ALU.subtract)
                    nc.gpsimd.tensor_tensor(rest[:, :, :], now, part[:, 0], ALU.subtract).then_inc(rest_ok, 1)
                    reach(pool, rest_ok, n, 1, 4)
                    nc.gpsimd.tensor_tensor(part[:, 2], rest[:, :, :], part[:, 1], ALU.subtract).then_inc(parts_ok, 1)
                if job == "rstd1" and n.has(5):
                    reach(pool, ve1_ok, n, 1, 6)
                    nc.gpsimd.tensor_tensor(rstd1[:, :], ve1[:, :], half_neg[:, :], ALU.pow).then_inc(rstd1_ok, 1)
                if job == "norm" and n.has(-2):
                    reach(pool, rb_in, n, 32, -1)
                    reach(pool, y_ps, n, 1, -2)
                    nc.gpsimd.tensor_tensor(ctxn[:, :, :], o_sb[:, n.ring(-2, 2)], rb[:, :, :], ALU.mult
                                            ).then_inc(norm_ok, 1)
                if job == "xb" and n.has(-2):
                    if n.c % 2 == 0:
                        reach(pool, xr_in, n, 8, 0)
                    reach(pool, x1_ok, n, 1, -2)
                    bias = bo_rows[int(n.second(-2))].unsqueeze(1).broadcast_to((128, TT, C))
                    nc.gpsimd.tensor_tensor(xb[:, :, :], xr[:, (n.c - 2) // 2 % 2, n.c % 2], bias, ALU.add
                                            ).then_inc(xb_ok, 1)
                if job == "x1b" and n.has(-3):
                    reach(pool, x2_ok, n, 1, -3)
                    nc.gpsimd.tensor_tensor(x1b[:, :, :], x1[:, :, :],
                                            bf_rows.unsqueeze(1).broadcast_to((128, TT, C)), ALU.add
                                            ).then_inc(x1b_ok, 1)
                if job == "rope" and n.has(4) and not n.second(4):
                    reach(pool, qk_ok, n, 1, 5)
                    nc.gpsimd.tensor_tensor(qk_cos[:, :, :], qk_raw[:, :, :], cos_t, ALU.mult)
                    nc.gpsimd.tensor_tensor(qk_swap[:, :, :], qk_swap[:, :, :], sin_t, ALU.mult).then_inc(rope_a, 1)
                    reach(pool, rope_a, n, 1, 5)
                    nc.gpsimd.tensor_tensor(qk[:, n.ring(4, 2)], qk_cos[:, :, :], qk_swap[:, :, :], ALU.add)
                    reach(pool, parts_out, n, 16, 4)
                    nc.gpsimd.tensor_tensor(part[:, 0], qk_cos[:, :, :], qk_swap[:, :, :], ALU.add
                                            ).then_inc(rope_ok, 1)
            def all_jobs(n):
                if n.c == FIRST + 1:
                    pool.wait_ge(consts_in, N_CONST)
                if n.c == 0 and n.i is None:
                    pool.wait_ge(setup_dve, 5)
                for job in POOL_ORDER:
                    step(n, job)
            steps(pool, all_jobs)

        @block.scalar
        def _(act):
            act.wait_ge(first_in, 16)
            act.wait_ge(setup_pool, N_FIXED)

            def qk_out(n, w, lot):
                src = small(n, "qk")[:, w * T:(w + 1) * T]
                if n.second(4):
                    to = part[:, 0, w] if lot == 1 else qk[:, n.ring(4, 2), w]
                    return nc.scalar.activation(to, src, ACT.Identity, scale=scal[:, w:w + 1],
                                                bias=cols[1][:, w:w + 1])
                if lot == 0:
                    return nc.scalar.activation(qk_raw[:, w], src, ACT.Identity, bias=cols[0][:, w:w + 1])
                to, of = (slice(0, 64), slice(64, 128)) if lot == 1 else (slice(64, 128), slice(0, 64))
                return nc.scalar.activation(qk_swap[to, w], src[of], ACT.Identity, bias=cols[0][of, w:w + 1])

            def step(n):
                for h in range(H):
                    if n.has(0):
                        u = h // 4
                        act.wait_ge(st_ps, n.lin(16, 0, h + 1))
                        if h % 4 == 0:
                            reach(act, pv_ps, n, 4, -1, u + 1)
                        nc.scalar.activation(pt[:, u, h % 4], ps_st[:, ST_BANK[h]], ACT.Exp,
                                             scale=float(D) ** -0.5).then_inc(exp_ok, 1)
                    if h == ACT_AT["xnT"] and n.has(4):
                        reach(act, xnT_ps, n, 1, 5)
                        reach(act, v_ps, n, 1, 1)
                        nc.scalar.activation(xnT[:, n.ring(4, 4)], small(n, "xnT")[:, 0:T], ACT.Copy
                                             ).then_inc(xnT_ok, 1)
                    if h == ACT_AT["mrow"] and n.has(1):
                        reach(act, mrow_ps, n, 1, 2)
                        reach(act, mrows_in, n, 16, 0)
                        nc.scalar.activation(mrow[:, n.ring(1, 2)], small(n, "mrow")[0:2 * H, 0:T], ACT.Copy
                                             ).then_inc(mrow_ok, 1)
                    if h == ACT_AT["o_sb"] and n.has(-1):
                        reach(act, pv_ps, n, 4, 0)
                        reach(act, norm_ok, n, 1, -2)
                        nc.scalar.activation(o_sb[:, n.ring(-1, 2)], ps_pv[:, :, :], ACT.Copy).then_inc(o_ok, 1)
                    for (w, lot), at in QK_OUT_AT[n.second(4)].items():
                        if h != at or not n.has(4):
                            continue
                        if (w, lot) == (0, 0):
                            reach(act, qk_ps, n, 1, 5)
                            if n.second(4):
                                reach(act, parts_ok, n, 1, 3)
                            else:
                                reach(act, rope_ok, n, 1, 4)
                        if n.second(4) and (w, lot) == (0, 1):
                            reach(act, parts_out, n, 16, 4)
                        last = qk_out(n, w, lot)
                        if (w, lot) == list(QK_OUT_AT[n.second(4)])[-1]:
                            last.then_inc(qk_ok, 1)
                    if h == ACT_AT["x1nT"] and n.has(-3):
                        reach(act, x1nT_ps, n, 1, -2)
                        reach(act, z_ps, n, 1, -3)
                        nc.scalar.activation(x1nT[:, :], small(n, "x1nT")[:, 0:T], ACT.Copy).then_inc(x1nT_ok, 1)
                    if h == ACT_AT["v"] and n.has(1):
                        reach(act, v_ps, n, 1, 2)
                        reach(act, pv_ps, n, 4, 0)
                        scale = scal[:, 2:3] if n.second(1) else 1.0
                        src = small(n, "v")[:, 0:TT * C].rearrange("p (s i h d) -> p s i h d", s=TT, i=2, h=8)
                        for i in range(2):
                            last = nc.scalar.activation(vpad[:, n.ring(1, 2), :, i, :, i:16:2], src[:, :, i],
                                                        ACT.Identity, scale=scale)
                        last.then_inc(v_ok, 1)
            steps(act, step)

        @block.vector
        def _(dve):
            def setup():
                dve.wait_ge(consts_in, N_CONST)
                dve.wait_ge(setup_pe, 1)
                nc.vector.tensor_copy(lo1[:, :], ps_pv[0:4, 0, 0:128]).then_inc(setup_dve, 1)
                nc.vector.tensor_copy(ident_bf[:, :], ident)
                for a in range(2):
                    nc.vector.tensor_copy(bv_rep[:, a], cols[a][:, 2:3].broadcast_to((128, 128)))
                dve.wait_ge(setup_pe, 2)
                nc.vector.tensor_copy(lo2[:, :], ps_pv[0:50, 0, 0:128]).then_inc(setup_dve, 1)
                dve.wait_ge(setup_pe, 3)
                nc.vector.tensor_tensor(wfT, ps_pv[:, 0, 0:128], wfT, ALU.add).then_inc(setup_dve, 1)
                dve.wait_ge(setup_pe, 4)
                nc.vector.tensor_tensor(bo_rows[0], ps_pv[:, 0, 0:128], bo_rows[0], ALU.add).then_inc(setup_dve, 1)
                nc.vector.scalar_tensor_tensor(bo_rows[1], ps_pv[:, 0, 128:256], scal[:, 3:4], bo_rows[1],
                                               ALU.mult, ALU.add).then_inc(setup_dve, 1)

            def statistics(x, stat, done, tile):
                last = nc.vector.bn_stats(stat[:, tile, :], x[:, tile, :])
                if tile == TT - 1:
                    last.then_inc(done, 1)

            def variance(stat, mv, ve, n, off, stats_sem, aggr_sem, ve_sem):
                for i in range(TT):
                    last = nc.vector.bn_aggr(mv[:, i, :], stat[:, i, :])
                last.then_inc(aggr_sem, 1)
                reach(dve, aggr_sem, n, 1, off, 1)
                nc.vector.tensor_scalar(ve[:, :], mv[:, :, 1], LN_EPS, None, ALU.add).then_inc(ve_sem, 1)

            def tiles(bank):
                return bank[:, 0:TT * C].rearrange("p (i c) -> p i c", i=TT)

            def step(n):
                if n.c == SETUP_STEP:
                    setup()
                xa_now = xa[:, (n.c + 5) // 2 % 2, (n.c + 5) % 2]
                for h in range(H):
                    if h == DVE_AT["var1"] and n.has(5):
                        reach(dve, stats1, n, 1, 6)
                    if h == DVE_AT["var2"] and n.has(-3):
                        reach(dve, stats2, n, 1, -2)
                    if n.has(2):
                        if h == 0:
                            reach(dve, mxp_ok, n, 1, 1)
                        dve.wait_ge(mx_ps, n.lin(16, 2, h + 1))
                        nc.vector.tensor_reduce(mx[:, n.ring(2, 2), :, h], ps_mx[:, h % 2], AX, ALU.max,
                                                negate=True).then_inc(mx_ok, 1)
                    if h == DVE_AT["mxp1"] and n.has(1):
                        reach(dve, mx_ok, n, 16, 2)
                        reach(dve, mrow_ps, n, 1, 1)
                        nc.vector.tensor_copy(mxp[:, :, 0], mx[:, n.ring(1, 2)]).then_inc(mxp1_ok, 1)
                    if h == DVE_AT["mxp2"] and n.has(1):
                        reach(dve, mxp1_ok, n, 1, 2)
                        nc.vector.tensor_tensor(mxp[:, :, 1], mx[:, n.ring(1, 2)], mxp[:, :, 0], ALU.subtract
                                                ).then_inc(mxp_ok, 1)
                    if h == DVE_AT["var2"] and n.has(-3):
                        variance(st2, mv2, ve2, n, -3, stats2, aggr2, ve2_ok)
                    for i in range(TT):
                        if h == DVE_AT[f"x1n_{i}"] and n.has(-3):
                            if i == 0:
                                reach(dve, rstd2_ok, n, 1, -2)
                                reach(dve, x1nT_ps, n, 1, -3)
                            last = nc.vector.tensor_scalar(x1n[:, i], x1[:, i], mv2[:, i, 0:1], rstd2[:, i:i + 1],
                                                           ALU.subtract, ALU.mult)
                            if i == 1:
                                last.then_inc(x1n_ok, 1)
                        if h == DVE_AT[f"st1_{i}"] and n.has(5):
                            if i == 0 and n.c % 2:
                                reach(dve, xa_in, n, 8, 7)
                            statistics(xa_now, st1, stats1, i)
                    if h == DVE_AT["var1"] and n.has(5):
                        variance(st1, mv1, ve1, n, 5, stats1, aggr1, ve1_ok)
                    for i in range(TT):
                        if h == DVE_AT[f"xn_{i}"] and n.has(5):
                            if i == 0:
                                reach(dve, rstd1_ok, n, 1, 6)
                                reach(dve, xnT_ps, n, 1, 5)
                            last = nc.vector.tensor_scalar(xn[:, i], xa_now[:, i], mv1[:, i, 0:1], rstd1[:, i:i + 1],
                                                           ALU.subtract, ALU.mult)
                            if i == 1:
                                last.then_inc(xn_ok, 1)
                    if h == DVE_AT["recip"] and n.has(-1):
                        reach(dve, rsum_in, n, 32, 0)
                        reach(dve, rinv_out, n, 16, -1)
                        nc.vector.reciprocal(rinv[:, :], rs[:, :]).then_inc(rinv_ok, 1)
                    if h == DVE_AT["x1"] and n.has(-2):
                        reach(dve, y_ps, n, 1, -1)
                        reach(dve, xb_ok, n, 1, -1)
                        reach(dve, x1b_ok, n, 1, -2)
                        y = tiles(small(n, "y"))
                        if n.second(-2):
                            nc.vector.scalar_tensor_tensor(x1[:, :, :], y, scal[:, 3:4], xb[:, :, :],
                                                           ALU.mult, ALU.add).then_inc(x1_ok, 1)
                        else:
                            nc.vector.tensor_tensor(x1[:, :, :], y, xb[:, :, :], ALU.add).then_inc(x1_ok, 1)
                    for i in range(TT):
                        if h == DVE_AT[f"st2_{i}"] and n.has(-2):
                            if i == 0:
                                reach(dve, x1_ok, n, 1, -1)
                            statistics(x1, st2, stats2, i)
                    if h == DVE_AT["x2"] and n.has(-4):
                        reach(dve, x1b_ok, n, 1, -3)
                        reach(dve, z_ps, n, 1, -3)
                        if n.c % 2 == 0:
                            reach(dve, x2_out, n, 8, -6)
                        nc.vector.tensor_tensor(x2[:, (n.c - 4) // 2 % 2, n.c % 2], tiles(small(n, "z")),
                                                x1b[:, :, :], ALU.add).then_inc(x2_ok, 1)
            steps(dve, step)

        @block.tensor
        def _(pe):
            mm = nc.tensor.matmul
            pe.wait_ge(first_in, 16)

            def setup():
                pe.wait_ge(consts_in, N_CONST)
                mm(ps_pv[0:4, 0, 0:128], lo_downT, aux_down, start=True, stop=True).then_inc(setup_pe, 1)
                pe.wait_ge(setup_dve, 1)
                mm(ps_pv[0:50, 0, 0:128], lo_upT, lo1[:, :], start=True, stop=True).then_inc(setup_pe, 1)
                pe.wait_ge(setup_dve, 2)
                mm(ps_pv[:, 0, 0:128], lo2[:, :], aux_upT, start=True, stop=True).then_inc(setup_pe, 1)
                pe.wait_ge(setup_dve, 3)
                for a in range(2):
                    last = mm(ps_pv[:, 0, a * 128:a * 128 + 128], bv_rep[:, a], woT[a], start=True, stop=True)
                last.then_inc(setup_pe, 1)
                pe.wait_ge(setup_dve, 5)
                pe.wait_ge(fill_in, 16)
                pe.wait_ge(setup_pool, N_FIXED)

            def key_major_scores(n, h):
                if h == 0:
                    reach(pe, mrows_in, n, 16, 1)
                reach(pe, exp_ok, n, 16, 0, ST_BEFORE[h] + 1)
                r = n.ring(0, 4)
                for s in range(TT):
                    last = mm(ps_st[:, ST_BANK[h], s], ks[0:KALL, r, h, s * 128:s * 128 + 128],
                              qs[0:KALL, r, h, :], start=True, stop=True)
                last.then_inc(st_ps, 1)

            def token_major_scores(n, h):
                if h == 0:
                    reach(pe, stacks_in, n, 96, 3)
                r = n.ring(2, 4)
                reach(pe, mx_ok, n, 16, 2, h - 1)
                for i in range(TT):
                    last = mm(ps_mx[:, h % 2, i], qs[0:KMAX, r, h, i * 128:i * 128 + 128],
                              ks[0:KMAX, r, h, :], start=True, stop=True)
                last.then_inc(mx_ps, 1)

            def times_v(n, off, u, s):
                i, r = u % 2, u // 2
                if s == 0:
                    reach(pe, exp_ok, n, 16, off, 4 * u + 4)
                    if u == 0:
                        reach(pe, v_ok, n, 1, off + 1)
                        reach(pe, o_ok, n, 1, off)
                for j in range(4):
                    last = mm(ps_pv[32 * j:32 * j + 32, r], vpad[:, n.ring(off, 2), s, i, r * 4 + j, :],
                              pt[:, u, j, s], start=(i == 0 and s == 0), stop=(i == 1 and s == 1))
                if s == 1:
                    last.then_inc(pv_ps, 1)

            def small_product(n, name, pieces):
                off, _ = SMALL[name]
                if not n.has(off):
                    return
                bank, a = small(n, name), int(n.second(off))
                if 0 in pieces:
                    small_bank_free(pe, n, name)
                if name == "xnT":
                    if 0 in pieces:
                        reach(pe, xn_ok, n, 1, 5)
                    for i in pieces:
                        last = nc.tensor.transpose(bank[:, i * 128:i * 128 + 128], xn[:, i], ident)
                    if 1 in pieces:
                        last.then_inc(xnT_ps, 1)
                if name == "mrow":
                    if 0 in pieces:
                        reach(pe, mxp_ok, n, 1, 2)
                    for i in pieces:
                        last = mm(bank[0:2 * H, i * 128:i * 128 + 128], mxp[:, i].rearrange("p a h -> p (a h)"),
                                  ident_bf[:, :], start=True, stop=True)
                    if 1 in pieces:
                        last.then_inc(mrow_ps, 1)
                if name == "qk":
                    if 0 in pieces:
                        reach(pe, xnT_ok, n, 1, 5)
                    for w in pieces:
                        last = mm(bank[:, w * T:(w + 1) * T], (wqT, wkT)[w][a], xnT[:, n.ring(4, 4)],
                                  start=True, stop=True)
                    if 1 in pieces:
                        last.then_inc(qk_ps, 1)
                if name == "x1nT":
                    if 0 in pieces:
                        reach(pe, x1n_ok, n, 1, -2)
                    for i in pieces:
                        last = nc.tensor.transpose(bank[:, i * 128:i * 128 + 128], x1n[:, i], ident)
                    if 1 in pieces:
                        last.then_inc(x1nT_ps, 1)
                if name == "y":
                    if 0 in pieces:
                        reach(pe, norm_ok, n, 1, -1)
                    for i in pieces:
                        for r in range(2):
                            last = mm(bank[:, i * C:i * C + C], ctxn[:, r, i * 128:i * 128 + 128], woP[a][r],
                                      start=(r == 0), stop=(r == 1))
                    if 1 in pieces:
                        last.then_inc(y_ps, 1)
                if name == "v":
                    for i in pieces:
                        last = mm(bank[:, i * C:i * C + C], xnT[:, n.ring(1, 4), i * 128:i * 128 + 128], wvT[a],
                                  start=True, stop=True)
                    if 1 in pieces:
                        last.then_inc(v_ps, 1)
                if name == "z":
                    if 0 in pieces:
                        reach(pe, x1nT_ok, n, 1, -3)
                    for i in pieces:
                        last = mm(bank[:, i * C:i * C + C], x1nT[:, i * 128:i * 128 + 128], wfT,
                                  start=True, stop=True)
                    if 1 in pieces:
                        last.then_inc(z_ps, 1)

            small_at = [("qk", (0,), PE_AT["q"]), ("qk", (1,), PE_AT["k"]), ("y", (0,), PE_AT["y0"]),
                        ("y", (1,), PE_AT["y1"])]
            small_at += [(name, (0, 1), PE_AT[name]) for name in ("z", "xnT", "mrow", "x1nT", "v")]

            def step(n):
                if n.c == SETUP_STEP:
                    setup()
                for h in range(H):
                    if n.has(0):
                        key_major_scores(n, h)
                    for name, pieces, at in small_at:
                        if h == at:
                            small_product(n, name, pieces)
                    if n.has(2):
                        token_major_scores(n, h)
                    for (u, s), at in QUADS_AT.items():
                        if h == at % H and n.has(-(at // H)):
                            times_v(n, -(at // H), u, s)
            steps(pe, step)


def kernel(**inputs):
    import numpy as np
    import concourse.bacc as bacc
    from concourse.bass_utils import run_bass_kernel_spmd

    g = {k: np.asarray(v) for k, v in inputs.items()}
    a, b, f = "L0_attn_a_", "L0_attn_b_", "L0_ffn_"
    names = [(a + "Wq", a + "Wk", a + "Wv", a + "Wo", a + "bq", a + "bk", a + "bv", a + "bo"),
             (b + "w_q", b + "w_k", b + "w_v", b + "w_o", b + "b_q", b + "b_k", b + "b_v", b + "b_o")]
    qk_order = np.array([8 * h + d for d in range(8) for h in range(16)])
    head = lambda i, r, j: 4 * (2 * r + i) + j
    v_order = np.array([8 * head(i, r, j) + d for i in range(2) for r in range(2) for j in range(4) for d in range(8)])
    inv_freq = (1.0 / 10000.0 ** (np.arange(0, 8, 2, dtype=np.float32) / 8)).astype(np.float32)
    angle = np.arange(256, dtype=np.float32)[None, :] * inv_freq[:, None]
    cos_t = np.repeat(np.cos(angle), 16, axis=0)
    sin_t = np.repeat(np.sin(angle), 16, axis=0)
    cos_t = np.concatenate([cos_t, cos_t]).astype(np.float32)
    sin_t = np.concatenate([-sin_t, sin_t]).astype(np.float32)
    fields = {
        "ident": np.eye(128, dtype=np.float32),
        "cos_t": np.concatenate([cos_t, cos_t], axis=1), "sin_t": np.concatenate([sin_t, sin_t], axis=1),
        "wfT": g[f + "W"].T, "lo_downT": g[f + "lora_down"].T, "aux_down": g[f + "down_aux"],
        "lo_upT": g[f + "lora_up"].T, "aux_upT": g[f + "up_aux"].T, "bf": g[f + "b"],
        "scal": np.stack([g[b + "s_q"], g[b + "s_k"], g[b + "s_v"], g[b + "s_o"]]).reshape(4),
    }
    for n, (wq, wk, wv, wo, bq, bk, bv, bo) in enumerate(names):
        fields[f"wqT{n}"] = g[wq][qk_order].T
        fields[f"wkT{n}"] = g[wk][qk_order].T
        fields[f"wvT{n}"] = g[wv][v_order].T
        fields[f"woT{n}"] = g[wo].T
        fields[f"cols{n}"] = np.stack([g[bq][qk_order], g[bk][qk_order], g[bv]], axis=1)
        fields[f"bo{n}"] = g[bo]
        for r in range(2):
            padded = np.zeros((128, 128), np.float32)
            for i in range(2):
                for j in range(4):
                    padded[32 * j + i:32 * j + 16:2] = g[wo].T[8 * head(i, r, j):8 * head(i, r, j) + 8]
            fields[f"woP{n}{r}"] = padded
    arrays = {"x": g[a + "x"],
              "ones": np.ones(H * T).astype(mybir.dt.np(mybir.dt.bfloat16))}
    for name, pack in PACKS.items():
        if name == "pack_rows":
            arrays[name] = np.concatenate([fields[field] for field, _, _ in pack])
            continue
        tile = np.zeros((128, sum(width for _, _, width in pack)), np.float32)
        at = 0
        for field, rows, width in pack:
            tile[0:rows, at:at + width] = fields[field]
            at += width
        arrays[name] = tile
    arrays = {f"in_{k}": np.ascontiguousarray(v) for k, v in arrays.items()}

    nc = bacc.Bacc("TRN2", target_bir_lowering=False, num_devices=1)
    io = {k[3:]: nc.dram_tensor(k, v.shape, mybir.dt.from_np(v.dtype), kind="ExternalInput").ap()
          for k, v in arrays.items()}
    out = nc.dram_tensor("out", (32, 256, 128), mybir.dt.float32, kind="ExternalOutput").ap()
    build(nc, io, out)
    r = run_bass_kernel_spmd(nc, [arrays], core_ids=[0])
    return r.results[0]["out"]
```
